# Optimizing a Trainium2 kernel written in Bass

```python
import numpy as np
import jax
import jax.numpy as jnp

def _softmax(x, axis=-1):
    return jax.nn.softmax(x, axis=axis)

def _gelu(x):
    return jax.nn.gelu(x, approximate=True)

def _silu(x):
    return jax.nn.silu(x)

def _sigmoid(x):
    return jax.nn.sigmoid(x)

def _layernorm(x, axis=-1, eps=1e-05):
    m = jnp.mean(x, axis=axis, keepdims=True)
    v = jnp.var(x, axis=axis, keepdims=True)
    return (x - m) / jnp.sqrt(v + eps)

def _scatter_add(tgt, idx, src, axis=0):
    return tgt.at[idx].add(src)

def _segment_sum(src, seg, n):
    return jax.ops.segment_sum(src, seg, n)
kernel_name = 'mk_adj_preln_d1_adj_r2_cb8bfc'

def setup_inputs(seed: int=0):
    np.random.seed(seed)
    _w = jnp.asarray

    def _rec_inputs():
        import jax
        import jax.numpy as jnp
        _gk = jax.random.key(seed)
        x = -0.0002928 + 1 * jax.random.normal(jax.random.fold_in(_gk, 1), (4096, 256), jnp.float32)
        _a = jax.random.bernoulli(jax.random.fold_in(_gk, 2), 0.000976562, (4096, 4096))
        adj = _a.astype(jnp.int32)
        return (x, adj)
    x, adj = _rec_inputs()

    def _L0_gnn_setup():
        import jax, jax.numpy as jnp
        import numpy as np
        N_X, N_NEIGH, D_IN, D_HID, D_OUT = (4096, 4096, 256, 32, 128)
        NEG_BIG = -9000000000000000.0
        key = jax.random.key(seed)
        ks = jax.random.split(key, 16)
        s_in = 1.0 / np.sqrt(D_IN)
        s_hid = 1.0 / np.sqrt(D_HID)
        return {'x': jax.random.normal(ks[0], (N_X, D_IN), jnp.float32), 'neigh': jax.random.normal(ks[1], (N_NEIGH, D_IN), jnp.float32), 'adj': jax.random.randint(ks[2], (N_X, N_NEIGH), 0, 2, jnp.int32), 'Wx1': jax.random.uniform(ks[3], (D_IN, D_HID), jnp.float32, -s_in, s_in), 'bx1': jnp.zeros((D_HID,), jnp.float32), 'Wx2': jax.random.uniform(ks[4], (D_HID, D_HID), jnp.float32, -s_hid, s_hid), 'bx2': jnp.zeros((D_HID,), jnp.float32), 'Wn1': jax.random.uniform(ks[5], (D_IN, D_HID), jnp.float32, -s_in, s_in), 'bn1': jnp.zeros((D_HID,), jnp.float32), 'Wn2': jax.random.uniform(ks[6], (D_HID, D_HID), jnp.float32, -s_hid, s_hid), 'bn2': jnp.zeros((D_HID,), jnp.float32), 'Wv': jax.random.uniform(ks[7], (D_IN, D_OUT), jnp.float32, -s_in, s_in), 'bv': jnp.zeros((D_OUT,), jnp.float32), 'Wfx': jax.random.uniform(ks[8], (D_IN, D_OUT), jnp.float32, -s_in, s_in), 'bfx': jnp.zeros((D_OUT,), jnp.float32)}
    _L0_gnn_all = _L0_gnn_setup()
    _L0_gnn_in = {k: v for k, v in _L0_gnn_all.items() if k in ('neigh', 'Wx1', 'bx1', 'Wx2', 'bx2', 'Wn1', 'bn1', 'Wn2', 'bn2', 'Wv', 'bv', 'Wfx', 'bfx')}
    del _L0_gnn_all
    return {'x': x, 'adj': adj, 'L0_gnn_neigh': _L0_gnn_in['neigh'], 'L0_gnn_Wx1': _L0_gnn_in['Wx1'], 'L0_gnn_bx1': _L0_gnn_in['bx1'], 'L0_gnn_Wx2': _L0_gnn_in['Wx2'], 'L0_gnn_bx2': _L0_gnn_in['bx2'], 'L0_gnn_Wn1': _L0_gnn_in['Wn1'], 'L0_gnn_bn1': _L0_gnn_in['bn1'], 'L0_gnn_Wn2': _L0_gnn_in['Wn2'], 'L0_gnn_bn2': _L0_gnn_in['bn2'], 'L0_gnn_Wv': _L0_gnn_in['Wv'], 'L0_gnn_bv': _L0_gnn_in['bv'], 'L0_gnn_Wfx': _L0_gnn_in['Wfx'], 'L0_gnn_bfx': _L0_gnn_in['bfx']}

def reference(x, adj, L0_gnn_neigh, L0_gnn_Wx1, L0_gnn_bx1, L0_gnn_Wx2, L0_gnn_bx2, L0_gnn_Wn1, L0_gnn_bn1, L0_gnn_Wn2, L0_gnn_bn2, L0_gnn_Wv, L0_gnn_bv, L0_gnn_Wfx, L0_gnn_bfx):
    import jax
    import jax.numpy as jnp

    def _L0_gnn_ref(x, neigh, adj, Wx1, bx1, Wx2, bx2, Wn1, bn1, Wn2, bn2, Wv, bv, Wfx, bfx):
        import jax, jax.numpy as jnp
        import numpy as np
        N_X, N_NEIGH, D_IN, D_HID, D_OUT = (4096, 4096, 256, 32, 128)
        NEG_BIG = -9000000000000000.0
        neib_att = jnp.tanh(neigh @ Wn1 + bn1) @ Wn2 + bn2
        value = neigh @ Wv + bv
        x_att = jnp.tanh(x @ Wx1 + bx1) @ Wx2 + bx2
        ws = jnp.einsum('nh,mh->nm', x_att, neib_att)
        ws = jax.nn.leaky_relu(ws, negative_slope=0.01)
        ws = jnp.where(adj > 0, ws, jnp.float32(NEG_BIG))
        ws = jax.nn.softmax(ws, axis=1)
        agg_neib = ws @ value
        out = jnp.concatenate([x @ Wfx + bfx, agg_neib], axis=1)
        return out
    h = jnp.maximum(_layernorm(x, axis=-1), 0.0)
    x = x + _L0_gnn_ref(h, L0_gnn_neigh, adj, L0_gnn_Wx1, L0_gnn_bx1, L0_gnn_Wx2, L0_gnn_bx2, L0_gnn_Wn1, L0_gnn_bn1, L0_gnn_Wn2, L0_gnn_bn2, L0_gnn_Wv, L0_gnn_bv, L0_gnn_Wfx, L0_gnn_bfx)
    return x

_drawn_inputs = setup_inputs


def setup_inputs(seed=0):
    import zlib

    import numpy as np

    out = dict(_drawn_inputs(seed))
    spreads = {'L0_gnn_bx1': (0.0, 2.0),
     'L0_gnn_bx2': (0.0, 0.585),
     'L0_gnn_bn1': (0.0, 2.0),
     'L0_gnn_bn2': (0.0, 2.0),
     'L0_gnn_bv': (0.0, 0.1),
     'L0_gnn_bfx': (0.0, 0.1)}
    factors = {'L0_gnn_Wx1': 8.0, 'L0_gnn_Wx2': 8.0, 'L0_gnn_Wn1': 8.0, 'L0_gnn_Wn2': 8.0}
    for name, (base, spread) in spreads.items():
        noise = np.random.default_rng([zlib.crc32(name.encode()), seed]).standard_normal(out[name].shape)
        drawn = base * np.exp(spread * noise) if base else spread * noise
        out[name] = jnp.asarray(drawn.astype(out[name].dtype))
    for name, factor in factors.items():
        out[name] = (out[name] * factor).astype(out[name].dtype)
    return out
```

```python
import concourse.bass as bass
from concourse import mybir
from contextlib import ExitStack


def preln_gnn(nc, x, adj, neigh, Wx1, bx1, Wx2, bx2, Wn1, bn1, Wn2, bn2, Wv, bv, Wfx, bfx, out):
    f32, bf16, i32 = mybir.dt.float32, mybir.dt.bfloat16, mybir.dt.int32
    ALU = mybir.AluOpType
    ACT = mybir.ActivationFunctionType
    AX = mybir.AxisListType

    P = 128
    N, D = x.shape
    M = neigh.shape[0]
    H = Wx1.shape[1]
    DO = Wv.shape[1]
    KD = D // P
    R = 4
    G = N // (P * R)
    GW = P * R
    TW = DO + H
    MC = M // P
    Q = M // 512
    BIG = float(2 ** 100)
    EPS = 1e-5
    assert N == M

    x_v = x.rearrange("(g p r) d -> g p r d", p=P, r=R)
    n_v = neigh.rearrange("(g p r) d -> g p r d", p=P, r=R)
    adj_v = adj.rearrange("(g p r) m -> g p r m", p=P, r=R)
    out_v = out.rearrange("(g p r) d -> g p r d", p=P, r=R)

    ctx = ExitStack()
    with ctx:
        def sb(name, shape, dt=f32):
            return ctx.enter_context(nc.sbuf_tensor(name, shape, dt))

        def sem(name):
            return ctx.enter_context(nc.semaphore(name))

        table = nc.dram_tensor("table", (M, TW), f32).ap()
        tab_w = table.rearrange("(g p r) d -> g p r d", p=P, r=R)
        tab_r = table.rearrange("(c p) d -> p c d", p=P)

        ident = sb("ident", [P, P])
        identb = sb("identb", [P, P], bf16)
        halfneg = sb("halfneg", [P, R])
        w1 = {s: sb(f"w1{s}", [P, KD, H]) for s in "nx"}
        w2 = {s: sb(f"w2{s}", [H, H]) for s in "nx"}
        ww = {s: sb(f"ww{s}", [P, KD, DO]) for s in "nx"}
        b1 = {s: sb(f"b1{s}", [H, 1]) for s in "nx"}
        b2x = sb("b2x", [H, 1])
        b2n = sb("b2n", [P, H])
        bvb = sb("bvb", [P, DO])
        bfb = sb("bfb", [P, DO])

        rows = [sb(f"rows{b}", [P, R, D]) for b in range(2)]
        hgrp = sb("hgrp", [P, R, D])
        rowsT = sb("rowsT", [P, KD, GW])
        tanhT = sb("tanhT", [H, GW])
        tab = [sb(f"tab{b}", [P, R, TW]) for b in range(2)]
        left = [sb(f"left{b}", [P, R, DO]) for b in range(2)]
        xbias = sb("xbias", [P, R, DO])
        stats = sb("stats", [P, R, 6])
        meanvar = sb("meanvar", [P, R, 2])
        vareps = sb("vareps", [P, R])
        rstd = sb("rstd", [P, R])
        shift = sb("shift", [P, R])
        xaT = sb("xaT", [H, N])

        adjt = [sb(f"adjt{b}", [P, M], i32) for b in range(2)]
        masked = sb("masked", [P, M], bf16)
        V = sb("V", [P, MC, DO])
        na = sb("na", [P, MC, H])
        naT = sb("naT", [H, M])
        xag = sb("xag", [H, GW])
        negpart = [sb(f"negpart{k}", [P, 512]) for k in range(2)]
        L = [sb(f"L{b}", [P, M]) for b in range(2)]
        cmax = sb("cmax", [P, Q])
        rmax = sb("rmax", [P, 1])
        nmax = sb("nmax", [P, 1])
        rsum = sb("rsum", [P, 1])
        rinv = sb("rinv", [P, 1])
        PT = [sb(f"PT{k}", [P, 512]) for k in range(2)]
        xres = sb("xres", [P, R, DO])
        right = [sb(f"right{b}", [P, R, DO]) for b in range(2)]

        bank = [ctx.enter_context(nc.psum_tensor(f"bank{k}", [P, 512], f32)) for k in range(8)]

        weights_loaded = sem("weights_loaded")
        zeroed = sem("zeroed")
        ident_ready = sem("ident_ready")
        consts_ready = sem("consts_ready")

        class Side:

            def __init__(self, s):
                self.name = s
                self.rows_loaded = [sem(f"rows_loaded_{s}{b}") for b in range(2)]
                self.T0_copied = sem(f"T0_copied_{s}")
                self.T1_copied = sem(f"T1_copied_{s}")
                self.transposed = sem(f"transposed_{s}")
                self.hidden = sem(f"hidden_{s}")
                self.tanh_ready = sem(f"tanh_ready_{s}")
                self.wide = sem(f"wide_{s}")
                self.second = sem(f"second_{s}")
                self.wide_copied = sem(f"wide_copied_{s}")
                self.second_copied = sem(f"second_copied_{s}")
                self.stored = [sem(f"stored_{s}{b}") for b in range(2)]

        nb, xs = Side("n"), Side("x")
        stats_ready = sem("stats_ready")
        var_ready = sem("var_ready")
        vareps_ready = sem("vareps_ready")
        rstd_ready = sem("rstd_ready")
        shift_ready = sem("shift_ready")
        h_ready = sem("h_ready")
        xbias_ready = sem("xbias_ready")

        d_table = sem("d_table")
        d_naT = sem("d_naT")
        d_naT_copied = sem("d_naT_copied")
        d_adj = [sem(f"d_adj{b}") for b in range(2)]
        d_mask = sem("d_mask")
        d_xag = sem("d_xag")
        d_score = sem("d_score")
        d_neg = sem("d_neg")
        d_leaky = sem("d_leaky")
        d_rmax = sem("d_rmax")
        d_nmax = sem("d_nmax")
        d_exp = sem("d_exp")
        d_xpose = sem("d_xpose")
        d_pt = [sem(f"d_pt{k}") for k in range(2)]
        d_agg = sem("d_agg")
        d_rinv = sem("d_rinv")
        d_xres = sem("d_xres")
        d_right = sem("d_right")
        d_stored = sem("d_stored")

        pe_gate, dve_gate, pool_gate = sem("pe_gate"), sem("dve_gate"), sem("pool_gate")

        psT = [bank[0], bank[1]]
        psH = bank[2]
        psW = [bank[3], bank[4]]
        psS = [bank[5], bank[6]]
        NW = 14

        block = ctx.enter_context(nc.Block())

        @block.sync
        def _(sp):
            def load(dst, src):
                sp.dma_start(dst, src).then_inc(weights_loaded, 16)

            sp.dma_start(rows[0][:], n_v[0]).then_inc(nb.rows_loaded[0], 16)
            for s, a, b_, c, d_, e in (("n", Wn1, Wn2, Wv, bn1, None), ("x", Wx1, Wx2, Wfx, bx1, None)):
                load(w1[s][:], a.rearrange("(k p) h -> p k h", p=P))
                load(w2[s][:], b_)
                load(ww[s][:], c.rearrange("(k p) h -> p k h", p=P))
                load(b1[s][:], d_.rearrange("(h a) -> h a", a=1))
            load(b2x[:], bx2.rearrange("(h a) -> h a", a=1))
            load(b2n[:], bn2.partition_broadcast(P))
            load(bvb[:], bv.partition_broadcast(P))
            load(bfb[:], bfx.partition_broadcast(P))
            sp.dma_start(rows[1][:], n_v[1]).then_inc(nb.rows_loaded[1], 16)

            with sp.Fori(0, G // 2 - 1) as it:
                for b in range(2):
                    sp.wait_ge(nb.transposed, 2 * (2 * it + b + 1))
                    sp.dma_start(rows[b][:], n_v[2 * it + 2 + b]).then_inc(nb.rows_loaded[b], 16)
            for b in range(2):
                sp.wait_ge(nb.transposed, 2 * (G - 1 + b))
                sp.dma_start(rows[b][:], x_v[b]).then_inc(xs.rows_loaded[b], 16)
            with sp.Fori(0, G // 2 - 1) as it:
                for b in range(2):
                    sp.wait_ge(h_ready, R * (2 * it + b + 1) + 1)
                    sp.wait_ge(xbias_ready, 2 * it + b + 1)
                    sp.dma_start(rows[b][:], x_v[2 * it + 2 + b]).then_inc(xs.rows_loaded[b], 16)

            for b in range(2):
                sp.wait_ge(nb.stored[b], 16 * (G // 2 + 1))
            sp.dma_start(V[:], tab_r[:, :, 0:DO]).then_inc(d_table, 16)
            sp.dma_start(na[:], tab_r[:, :, DO:TW]).then_inc(d_table, 16)
            for r in range(2):
                sp.dma_start(adjt[r][:], adj_v[0, :, r, :]).then_inc(d_adj[r], 16)

            def dense_loads(g, last):
                sp.wait_ge(d_right, R * g + 1)
                sp.dma_start(xres[:], x_v[g, :, :, DO:D]).then_inc(d_xres, 16)
                for r in range(2, R):
                    sp.wait_ge(d_mask, R * g + r - 1)
                    sp.dma_start(adjt[r % 2][:], adj_v[g, :, r, :]).then_inc(d_adj[r % 2], 16)
                for r in range(0 if last else 2):
                    sp.wait_ge(d_mask, R * g + r + 3)
                    sp.dma_start(adjt[r][:], adj_v[g + 1, :, r, :]).then_inc(d_adj[r], 16)

            with sp.Fori(0, G - 1) as g:
                dense_loads(g, False)
            dense_loads(G - 1, True)

        @block.gpsimd
        def _(pool):
            nc.gpsimd.memset(ident[:], 0.0).then_inc(zeroed, 1)
            nc.gpsimd.memset(identb[:], 0.0).then_inc(zeroed, 1)
            nc.gpsimd.memset(halfneg[:], -0.5).then_inc(consts_ready, 1)
            pool.wait_ge(zeroed, 2)
            for m in (ident, identb):
                nc.gpsimd.affine_select(out=m[:], in_=m[:], compare_op=ALU.not_equal, fill=1.0, base=0,
                                        pattern=[[-1, P]], channel_multiplier=1).then_inc(ident_ready, 1)
            pool.wait_ge(weights_loaded, 16 * 12)
            pool.wait_ge(consts_ready, 1)
            with pool.Fori(0, G // 2) as it:
                for b in range(2):
                    j = 2 * it + b
                    pool.wait_ge(xs.rows_loaded[b], 16 * (it + 1))
                    pool.wait_ge(xs.wide_copied, j + 1)
                    nc.gpsimd.tensor_tensor(xbias[:], rows[b][:, :, 0:DO],
                                            bfb[:].unsqueeze(1).to_broadcast([P, R, DO]),
                                            ALU.add).then_inc(xbias_ready, 1)
                    pool.wait_ge(var_ready, R * (j + 1))
                    pool.wait_ge(shift_ready, j + 1)
                    pool.sem_inc(pool_gate, 1)
                    nc.gpsimd.tensor_scalar(vareps[:], meanvar[:, :, 1], EPS, None, ALU.add).then_inc(vareps_ready, 1)
                    pool.wait_ge(vareps_ready, j + 1)
                    pool.wait_ge(h_ready, R * j + 1)
                    nc.gpsimd.tensor_tensor(rstd[:], vareps[:], halfneg[:], ALU.pow).then_inc(rstd_ready, 1)

        @block.tensor
        def _(pe):
            def transposes(sd, j, src):
                for k, copied in enumerate((sd.T0_copied, sd.T1_copied)):
                    pe.wait_ge(copied, j + 1)
                    for r in range(R):
                        last = nc.tensor.transpose(psT[k][:, r * P:(r + 1) * P], src[:, r, k * P:(k + 1) * P], ident[:])
                    last.then_inc(sd.transposed, 1)

            def hidden(sd, j):
                pe.wait_ge(sd.T0_copied, j + 2)
                pe.wait_ge(sd.T1_copied, j + 2)
                pe.wait_ge(sd.tanh_ready, j + 1)
                for k in range(KD):
                    last = nc.tensor.matmul(psH[0:H, :], w1[sd.name][:, k, :], rowsT[:, k, :],
                                            start=k == 0, stop=k == KD - 1)
                last.then_inc(sd.hidden, 1)

            def wide(sd, j, b):
                pe.wait_ge(sd.wide_copied, j + 1)
                for r in range(R):
                    for k in range(KD):
                        last = nc.tensor.matmul(psW[b][:, r * DO:(r + 1) * DO], rowsT[:, k, r * P:(r + 1) * P],
                                                ww[sd.name][:, k, :], start=k == 0, stop=k == KD - 1)
                last.then_inc(sd.wide, 1)

            pe.wait_ge(ident_ready, 2)
            pe.wait_ge(weights_loaded, 16 * 12)
            with pe.Fori(0, G // 2) as it:
                for b in range(2):
                    j = 2 * it + b
                    pe.wait_ge(nb.rows_loaded[b], 16 * (it + 1))
                    transposes(nb, j, rows[b])
                    hidden(nb, j)
                    wide(nb, j, b)
                    pe.wait_ge(nb.tanh_ready, j + 2)
                    pe.wait_ge(nb.second_copied, j + 1)
                    pe.sem_inc(pe_gate, 1)
                    for r in range(R):
                        last = nc.tensor.matmul(psS[b][:, r * H:(r + 1) * H], tanhT[:, r * P:(r + 1) * P], w2["n"][:],
                                                start=True, stop=True)
                    last.then_inc(nb.second, 1)
            pe.wait_ge(nb.wide_copied, G + 1)
            pe.wait_ge(nb.second_copied, G + 1)
            with pe.Fori(0, G // 2) as it:
                for b in range(2):
                    j = 2 * it + b
                    pe.wait_ge(h_ready, R * (j + 1) + 1)
                    transposes(xs, j, hgrp)
                    hidden(xs, j)
                    wide(xs, j, b)
                    pe.wait_ge(xs.tanh_ready, j + 2)
                    pe.wait_ge(xs.second_copied, j + 1)
                    pe.sem_inc(pe_gate, 1)
                    nc.tensor.matmul(psS[b][0:H, :], w2["x"][:], tanhT[:], start=True, stop=True).then_inc(xs.second, 1)

            pe.wait_ge(xs.wide_copied, G + 1)
            pe.wait_ge(xs.second_copied, G + 1)
            pe.wait_ge(d_table, 32)
            for q in range(Q):
                if q >= 2:
                    pe.wait_ge(d_naT_copied, q - 1)
                for c in range(4):
                    last = nc.tensor.transpose(bank[q % 2][0:H, c * P:(c + 1) * P], na[:, 4 * q + c, :], ident[:])
                last.then_inc(d_naT, 1)
            pe.wait_ge(d_naT_copied, Q)

            with pe.Fori(0, G) as g:
                pe.wait_ge(d_xag, g + 1)
                for r in range(R):
                    t = R * g + r
                    pe.wait_ge(d_mask, t + 1)
                    for q in range(Q):
                        pe.wait_ge(d_leaky, Q * t + q + 1)
                        nc.tensor.matmul(bank[q % 2][:], identb[:], masked[:, q * 512:(q + 1) * 512], start=True, stop=False)
                        nc.tensor.matmul(bank[q % 2][:], xag[:, r * P:(r + 1) * P], naT[:, q * 512:(q + 1) * 512],
                                         start=False, stop=True).then_inc(d_score, 1)

                    def weights_T(u):
                        pe.wait_ge(d_pt[u % 2], (Q // 2) * t + u // 2 + 1)
                        for c in range(4):
                            last = nc.tensor.transpose(bank[2 + u % 2][:, c * P:(c + 1) * P],
                                                       L[r % 2][:, (4 * u + c) * P:(4 * u + c + 1) * P], ident[:])
                        last.then_inc(d_xpose, 1)

                    pe.wait_ge(d_exp, t + 1)
                    pe.wait_ge(d_right, t + 1)
                    weights_T(0)
                    for u in range(Q):
                        if u + 1 < Q:
                            weights_T(u + 1)
                        pe.wait_ge(d_pt[u % 2], (Q // 2) * t + u // 2 + 2)
                        for c in range(4):
                            last = nc.tensor.matmul(bank[4][:, 0:DO], PT[u % 2][:, c * P:(c + 1) * P], V[:, 4 * u + c, :],
                                                    start=(u == 0 and c == 0), stop=(u == Q - 1 and c == 3))
                    last.then_inc(d_agg, 1)

        @block.scalar
        def _(act):
            for s in (nb.T0_copied, nb.tanh_ready, xs.T0_copied, xs.tanh_ready, xs.second_copied, h_ready):
                act.sem_inc(s, 1)
            act.wait_ge(weights_loaded, 16 * 12)
            for b in range(2):
                act.sem_inc(nb.stored[b], 16)
                act.sem_inc(xs.stored[b], 16)
            with act.Fori(0, G // 2) as it:
              for b in range(2):
                j = 2 * it + b
                act.wait_ge(nb.transposed, 2 * j + 1)
                nc.scalar.activation(rowsT[:, 0, :], psT[0][:], ACT.Copy).then_inc(nb.T0_copied, 1)
                act.wait_ge(nb.hidden, j + 1)
                nc.scalar.activation(tanhT[:], psH[0:H, :], ACT.Tanh, bias=b1["n"][:]).then_inc(nb.tanh_ready, 1)
                act.wait_ge(nb.wide, j + 1)
                act.wait_ge(nb.second, j + 1)
                act.wait_ge(nb.wide_copied, j + 2)
                act.wait_ge(nb.second_copied, j + 2)
                act.dma_start(tab_w[j], tab[b][:]).then_inc(nb.stored[b], 16)
            with act.Fori(0, G // 2) as it:
                for b in range(2):
                    j = 2 * it + b
                    act.wait_ge(shift_ready, j + 2)
                    for r in range(R):
                        nc.scalar.activation(hgrp[:, r, :], rows[b][:, r, :], ACT.Relu, scale=rstd[:, r:r + 1],
                                             bias=shift[:, r:r + 1]).then_inc(h_ready, 1)
                    act.wait_ge(xs.transposed, 2 * j + 1)
                    nc.scalar.activation(rowsT[:, 0, :], psT[0][:], ACT.Copy).then_inc(xs.T0_copied, 1)
                    act.wait_ge(xs.hidden, j + 1)
                    nc.scalar.activation(tanhT[:], psH[0:H, :], ACT.Tanh, bias=b1["x"][:]).then_inc(xs.tanh_ready, 1)
                    act.wait_ge(xs.second, j + 1)
                    nc.scalar.activation(xaT[:, bass.ds(j * GW, GW)], psS[b][0:H, :], ACT.Identity,
                                         bias=b2x[:]).then_inc(xs.second_copied, 1)
                    act.wait_ge(xs.wide_copied, j + 2)
                    act.dma_start(out_v[j, :, :, 0:DO], left[b][:]).then_inc(xs.stored[b], 16)
            for b in range(2):
                act.wait_ge(xs.stored[b], 16 * (G // 2 + 1))

            act.sem_inc(d_pt[0], 1)
            act.sem_inc(d_stored, 16)
            act.wait_ge(xs.second_copied, G + 1)
            with act.Fori(0, G) as g:
                nc.scalar.activation(xag[:], xaT[:, bass.ds(g * GW, GW)], ACT.Copy).then_inc(d_xag, 1)
                for r in range(R):
                    t = R * g + r
                    for q in range(Q):
                        act.wait_ge(d_score, Q * t + q + 1)
                        act.wait_ge(d_leaky, Q * t + q + 1)
                        nc.scalar.activation(negpart[q % 2][:], bank[q % 2][:], ACT.Relu, scale=-0.99).then_inc(d_neg, 1)
                    act.wait_ge(d_nmax, t + 1)
                    act.wait_ge(d_rinv, t + 1)
                    nc.scalar.activation(L[r % 2][:], L[r % 2][:], ACT.Exp, bias=nmax[:],
                                         accum_out=rsum[:]).then_inc(d_exp, 1)
                    for u in range(0, Q, 2):
                        act.wait_ge(d_xpose, Q * t + u + 1)
                        nc.scalar.activation(PT[0][:], bank[2][:], ACT.Copy).then_inc(d_pt[0], 1)
                act.wait_ge(d_right, R * (g + 1) + 1)
                act.dma_start(out_v[g, :, :, DO:D], right[0][:]).then_inc(d_stored, 16)
            act.wait_ge(d_stored, 16 * (G + 1))

        @block.vector
        def _(dve):
            for s in (nb.T1_copied, nb.wide_copied, nb.second_copied, xs.T1_copied, xs.wide_copied, shift_ready):
                dve.sem_inc(s, 1)
            dve.wait_ge(weights_loaded, 16 * 12)
            with dve.Fori(0, G // 2) as it:
                for b in range(2):
                    j = 2 * it + b
                    dve.wait_ge(nb.transposed, 2 * j + 2)
                    nc.vector.tensor_copy(rowsT[:, 1, :], psT[1][:]).then_inc(nb.T1_copied, 1)
                    dve.wait_ge(nb.wide, j + 1)
                    dve.wait_ge(nb.stored[b], 16 * (it + 1))
                    nc.vector.tensor_tensor(tab[b][:, :, 0:DO], psW[b][:].rearrange("p (r d) -> p r d", r=R),
                                            bvb[:].unsqueeze(1).to_broadcast([P, R, DO]), ALU.add).then_inc(nb.wide_copied, 1)
                    dve.wait_ge(nb.second, j + 1)
                    nc.vector.tensor_tensor(tab[b][:, :, DO:TW], psS[b][:, 0:R * H].rearrange("p (r d) -> p r d", r=R),
                                            b2n[:].unsqueeze(1).to_broadcast([P, R, H]), ALU.add).then_inc(nb.second_copied, 1)
            with dve.Fori(0, G // 2) as it:
                for b in range(2):
                    j = 2 * it + b
                    dve.wait_ge(xs.rows_loaded[b], 16 * (it + 1))
                    for r in range(R):
                        nc.vector.bn_stats(stats[:, r, :], rows[b][:, r, :]).then_inc(stats_ready, 1)
                    dve.wait_ge(stats_ready, R * (j + 1))
                    dve.sem_inc(dve_gate, 1)
                    for r in range(R):
                        nc.vector.bn_aggr(meanvar[:, r, :], stats[:, r, :]).then_inc(var_ready, 1)
                    dve.wait_ge(rstd_ready, j + 1)
                    dve.wait_ge(var_ready, R * (j + 1))
                    nc.vector.scalar_tensor_tensor(shift[:], meanvar[:, :, 0], -1.0, rstd[:], ALU.mult,
                                                   ALU.mult).then_inc(shift_ready, 1)
                    dve.wait_ge(xs.transposed, 2 * j + 2)
                    nc.vector.tensor_copy(rowsT[:, 1, :], psT[1][:]).then_inc(xs.T1_copied, 1)
                    dve.wait_ge(xs.wide, j + 1)
                    dve.wait_ge(xbias_ready, j + 1)
                    dve.wait_ge(xs.stored[b], 16 * (it + 1))
                    nc.vector.tensor_tensor(left[b][:], psW[b][:].rearrange("p (r d) -> p r d", r=R), xbias[:],
                                            ALU.add).then_inc(xs.wide_copied, 1)

            dve.sem_inc(d_leaky, 2)
            dve.sem_inc(d_pt[1], 1)
            dve.sem_inc(d_right, 1)
            dve.sem_inc(d_rinv, 1)
            for q in range(Q):
                dve.wait_ge(d_naT, q + 1)
                nc.vector.tensor_copy(naT[:, q * 512:(q + 1) * 512], bank[q % 2][0:H, :]).then_inc(d_naT_copied, 1)
            with dve.Fori(0, G) as g:
                for r in range(R):
                    t = R * g + r
                    dve.wait_ge(d_adj[r % 2], 32 * g + 16 * (r // 2) + 16)
                    nc.vector.tensor_scalar(masked[:], adjt[r % 2][:], 0.0, -BIG, ALU.is_le, ALU.mult).then_inc(d_mask, 1)
                    for q in range(Q):
                        dve.wait_ge(d_neg, Q * t + q + 1)
                        dve.sem_inc(dve_gate, 1)
                        nc.vector.tensor_tensor_reduce(out=L[r % 2][:, q * 512:(q + 1) * 512], in0=bank[q % 2][:],
                                                       in1=negpart[q % 2][:], scale=1.0, scalar=-3.0e38,
                                                       op0=ALU.add, op1=ALU.max,
                                                       accum_out=cmax[:, q:q + 1]).then_inc(d_leaky, 1)
                    dve.wait_ge(d_leaky, Q * (t + 1) + 2)
                    nc.vector.tensor_reduce(rmax[:], cmax[:], AX.X, ALU.max).then_inc(d_rmax, 1)
                    dve.wait_ge(d_rmax, t + 1)
                    nc.vector.tensor_scalar(nmax[:], rmax[:], -1.0, None, ALU.mult).then_inc(d_nmax, 1)
                    for u in range(1, Q, 2):
                        dve.wait_ge(d_xpose, Q * t + u + 1)
                        nc.vector.tensor_copy(PT[1][:], bank[3][:]).then_inc(d_pt[1], 1)
                    dve.wait_ge(d_exp, t + 1)
                    nc.vector.reciprocal(rinv[:], rsum[:]).then_inc(d_rinv, 1)
                    dve.wait_ge(d_agg, t + 1)
                    dve.wait_ge(d_rinv, t + 2)
                    if r == 0:
                        dve.wait_ge(d_xres, 16 * (g + 1))
                        dve.wait_ge(d_stored, 16 * (g + 1))
                    nc.vector.scalar_tensor_tensor(right[0][:, r, :], bank[4][:, 0:DO], rinv[:], xres[:, r, :],
                                                   ALU.mult, ALU.add).then_inc(d_right, 1)


_INS = ["x", "adj"] + ["L0_gnn_" + n for n in
        ("neigh", "Wx1", "bx1", "Wx2", "bx2", "Wn1", "bn1", "Wn2", "bn2", "Wv", "bv", "Wfx", "bfx")]


def kernel(**inputs):
    import numpy as np
    import concourse.bacc as bacc
    from concourse.bass_utils import run_bass_kernel_spmd

    nc = bacc.Bacc("TRN2", target_bir_lowering=False, num_devices=1)
    arrays, args = {}, []
    for name in _INS:
        a = np.ascontiguousarray(inputs[name])
        arrays[name] = a
        args.append(nc.dram_tensor(name, a.shape, mybir.dt.from_np(a.dtype), kind="ExternalInput").ap())
    args.append(nc.dram_tensor("out", arrays["x"].shape, mybir.dt.float32, kind="ExternalOutput").ap())
    preln_gnn(nc, *args)
    return run_bass_kernel_spmd(nc, [arrays], core_ids=[0]).results[0]["out"]
```

```python
import concourse.bass as bass
from concourse import mybir
from contextlib import ExitStack


def preln_gnn(nc, x, adj, neigh, Wx1, bx1, Wx2, bx2, Wn1, bn1, Wn2, bn2, Wv, bv, Wfx, bfx, out):
    f32, bf16, f16, i32, u32 = (mybir.dt.float32, mybir.dt.bfloat16, mybir.dt.float16, mybir.dt.int32,
                                mybir.dt.uint32)
    ALU = mybir.AluOpType
    ACT = mybir.ActivationFunctionType
    AX = mybir.AxisListType

    P = 128
    N, D = x.shape
    M = neigh.shape[0]
    H = Wx1.shape[1]
    DO = Wv.shape[1]
    KD = D // P
    R = 4
    G = N // (P * R)
    NT = N // P
    GW = P * R
    TW = DO + H
    MC = M // P
    Q = M // 512
    BIG = float(2 ** 100)
    EPS = 1e-5

    NQ = 4
    QW = M // NQ
    QP = QW + 8
    S = NQ * 8
    SS = S + 1
    C = 5
    E = C * P
    NONE = 8192
    assert N == M and KD == 2

    x_v = x.rearrange("(g p r) d -> g p r d", p=P, r=R)
    n_v = neigh.rearrange("(g p r) d -> g p r d", p=P, r=R)
    adj_v = adj.rearrange("(g p r) m -> g p r m", p=P, r=R)
    adj_q = adj.rearrange("(g p r) (q w) -> g p r q w", p=P, r=R, q=NQ)
    out_v = out.rearrange("(g p r) d -> g p r d", p=P, r=R)

    ctx = ExitStack()
    with ctx:
        def sb(name, shape, dt=f32):
            return ctx.enter_context(nc.sbuf_tensor(name, shape, dt))

        def sem(name):
            return ctx.enter_context(nc.semaphore(name))

        table = nc.dram_tensor("table", (M + 1, TW), f32).ap()
        tab_w = table[0:M].rearrange("(g p r) d -> g p r d", p=P, r=R)
        tab_r = table[0:M].rearrange("(c p) d -> p c d", p=P)

        ident = sb("ident", [P, P])
        identb = sb("identb", [P, P], bf16)
        before = sb("before", [P, P], bf16)
        upto = sb("upto", [P, P], bf16)
        nextdiff = sb("nextdiff", [P, P], bf16)
        maskdiff = sb("maskdiff", [P, P], bf16)
        maskrow = sb("maskrow", [P, P], bf16)
        firstrow = sb("firstrow", [P, P], bf16)
        onesb = sb("onesb", [P, 512], bf16)
        onesf = sb("onesf", [P, P])
        meanw = sb("meanw", [P, 1])
        colno = sb("colno", [P, E])
        colid = sb("colid", [P, C])
        quarter = sb("quarter", [P, 2 * SS], f16)
        ones_i = sb("ones_i", [P, 8], i32)
        onesS = sb("onesS", [P, S])
        halfneg = sb("halfneg", [P, R])
        w1 = {s: sb(f"w1{s}", [P, KD, H]) for s in "nx"}
        w2 = {s: sb(f"w2{s}", [H, H]) for s in "nx"}
        ww = {s: sb(f"ww{s}", [P, KD, DO]) for s in "nx"}
        b1 = {s: sb(f"b1{s}", [H, 1]) for s in "nx"}
        b2x = sb("b2x", [H, 1])
        b2n = sb("b2n", [P, H])
        bvb = sb("bvb", [P, DO])
        bfb = sb("bfb", [P, DO])

        rows = [sb(f"rows{b}", [P, R, D]) for b in range(2)]
        hgrp = sb("hgrp", [P, R, D])
        rowsT = [sb(f"rowsT{b}", [P, KD, GW]) for b in range(2)]
        tanhT = sb("tanhT", [H, GW])
        tab = [sb(f"tab{b}", [P, R, TW]) for b in range(2)]
        vsum = sb("vsum", [P, R, DO])
        vmean = sb("vmean", [1, TW])
        left = [sb(f"left{b}", [P, R, DO]) for b in range(2)]
        xbias = sb("xbias", [P, R, DO])
        stats = sb("stats", [P, R, 6])
        meanvar = sb("meanvar", [P, R, 2])
        vareps = sb("vareps", [P, R])
        rstd = sb("rstd", [P, R])
        shift = sb("shift", [P, R])
        xaT = sb("xaT", [H, N])
        xright = sb("xright", [P, NT, DO])

        adjt = [sb(f"adjt{r}", [P, NQ, QP], i32) for r in range(R)]
        found = [sb(f"found{b}", [P, S], u32) for b in range(2)]
        valid = sb("valid", [P, NT, SS])
        places = sb("places", [P, NT, 2 * SS], f16)
        adjsum = sb("adjsum", [P, NT, 2])
        sink = sb("sink", [P, 2, QW], bf16)
        cum = [sb(f"cum{b}", [P, SS]) for b in range(2)]
        total = [sb(f"total{b}", [P, 1], bf16) for b in range(2)]
        passed = [sb(f"passed{r}", [P, E], bf16) for r in range(R)]
        diffs = sb("diffs", [P, 2 * SS], f16)
        match = sb("match", [P, C, SS])
        hit = sb("hit", [P, C, SS])
        hitsum = sb("hitsum", [P, C])
        index = [sb(f"index{r}", [P, C], u32) for r in range(R)]

        cols = [sb(f"cols{r}", [P, C, TW]) for r in range(R)]
        xat = [sb(f"xat{r}", [H, P]) for r in range(R)]
        colsT = sb("colsT", [H, E])
        neg = sb("neg", [P, E])
        prob = [sb(f"prob{b}", [P, E]) for b in range(2)]
        probT = sb("probT", [P, E])
        smax = [sb(f"smax{b}", [P, 1]) for b in range(2)]
        snmax = [sb(f"snmax{b}", [P, 1]) for b in range(2)]
        ssum = [sb(f"ssum{b}", [P, 1]) for b in range(2)]
        sinv = sb("sinv", [P, 1])

        counts = sb("counts", [P, NT])
        sums = sb("sums", [P, NT])
        slots = sb("slots", [P, NT])
        bad = sb("bad", [P, 2, NT])
        badsum = sb("badsum", [P, 1])
        flag = sb("flag", [1, 1], i32)

        d_adjt = [adjt[b][:].rearrange("p q w -> p (q w)")[:, 0:M] for b in range(2)]
        L = adjt[2][:].rearrange("p q w -> p (q w)")[:, 0:M].bitcast(f32)
        masked = adjt[3][:].rearrange("p q w -> p (q w)")[:, 0:M // 2].bitcast(bf16)
        naT = sb("naT", [H, M])
        V = xright
        na = hgrp[:].rearrange("p r d -> p (r d)").rearrange("p (c h) -> p c h", h=H)
        xag = tanhT
        negpart = [rowsT[0][:, k, :] for k in range(2)]
        PT = [rowsT[1][:, k, :] for k in range(2)]
        cmax = sb("cmax", [P, Q])
        rmax = sb("rmax", [P, 1])
        nmax = sb("nmax", [P, 1])
        rsum = sb("rsum", [P, 1])
        rinv = sb("rinv", [P, 1])
        xres = left[0]
        right = left[1]

        bankA = ctx.enter_context(nc.psum_tensor("bankA", [P, 1024], f32))
        bankB = ctx.enter_context(nc.psum_tensor("bankB", [P, 1024], f32))
        bankC = ctx.enter_context(nc.psum_tensor("bankC", [P, 1024], f32))
        bankD = ctx.enter_context(nc.psum_tensor("bankD", [P, 512], f32))
        bankF = ctx.enter_context(nc.psum_tensor("bankF", [P, 512], f32))
        psT = [bankA[:, 0:512], bankA[:, 512:1024]]
        psH = bankF[:]
        psW = [bankB[:, 0:512], bankB[:, 512:1024]]
        psS = [bankC[:, 0:512], bankC[:, 512:1024]]
        psStart, psEnd = bankD[:, 336:337], bankD[:, 337:338]
        psDiff = bankD[:, 340:340 + 2 * SS]
        psPick = bankD[:, 0:C * 2 * SS].rearrange("p (c s) -> p c s", c=C)
        psColsT = bankA[0:H, 0:E]
        psScore = bankB[:, 0:E]
        psProbT = bankC[:, 0:E]
        psOut = bankF[:, 0:DO]
        psCheck = bankF[:, 256:256 + NT]
        psMean = bankF[0:1, 384:384 + DO]
        dbank = [bankA[:, 0:512], bankA[:, 512:1024], bankB[:, 0:512], bankB[:, 512:1024], bankF[:]]

        weights_loaded = sem("weights_loaded")
        NVC = 6 + R
        NWL = 12
        filled = sem("filled")
        consts_ready = sem("consts_ready")
        vec_consts = sem("vec_consts")

        class Side:

            def __init__(self, s):
                self.name = s
                self.rows_loaded = [sem(f"rows_loaded_{s}{b}") for b in range(2)]
                self.T0_copied = sem(f"T0_copied_{s}")
                self.T1_copied = sem(f"T1_copied_{s}")
                self.transposed = sem(f"transposed_{s}")
                self.hidden = sem(f"hidden_{s}")
                self.tanh_ready = sem(f"tanh_ready_{s}")
                self.wide = sem(f"wide_{s}")
                self.second = sem(f"second_{s}")
                self.wide_copied = sem(f"wide_copied_{s}")
                self.second_copied = sem(f"second_copied_{s}")
                self.stored = [sem(f"stored_{s}{b}") for b in range(2)]

        nb, xs = Side("n"), Side("x")
        vsum_added = sem("vsum_added")
        mean_ready = sem("mean_ready")
        vmean_copied = sem("vmean_copied")
        mean_stored = sem("mean_stored")
        stats_ready = sem("stats_ready")
        var_ready = sem("var_ready")
        vareps_ready = sem("vareps_ready")
        rstd_ready = sem("rstd_ready")
        shift_ready = sem("shift_ready")
        h_ready = sem("h_ready")
        xbias_ready = sem("xbias_ready")
        xright_loaded = sem("xright_loaded")

        adj_loaded = [sem(f"adj_loaded{r}") for r in range(R)]
        quarter_found = sem("quarter_found")
        adj_summed = sem("adj_summed")
        valid_ready = sem("valid_ready")
        value_ready = sem("value_ready")
        scanned = sem("scanned")
        spare_valid = sem("spare_valid")
        spare_cum = sem("spare_cum")
        total_ready = sem("total_ready")
        ends_ready = sem("ends_ready")
        places_ready = sem("places_ready")
        passed_ready = sem("passed_ready")
        diff_made = sem("diff_made")
        diffs_copied = sem("diffs_copied")
        picked = sem("picked")
        matched = sem("matched")
        hit_ready = sem("hit_ready")
        hits_summed = sem("hits_summed")
        index_ready = sem("index_ready")
        gathered = [sem(f"gathered{r}") for r in range(R)]
        xat_ready = sem("xat_ready")

        colsT_made = sem("colsT_made")
        colsT_copied = sem("colsT_copied")
        scored = sem("scored")
        neg_ready = sem("neg_ready")
        leaky_ready = sem("leaky_ready")
        nmax_ready = sem("nmax_ready")
        exp_ready = sem("exp_ready")
        probT_made = sem("probT_made")
        probT_copied = sem("probT_copied")
        summed_up = sem("summed_up")
        sinv_ready = sem("sinv_ready")
        result_ready = sem("result_ready")
        result_stored = sem("result_stored")

        check_step = sem("check_step")
        check_sum = sem("check_sum")
        flag_ready = sem("flag_ready")

        d_table = sem("d_table")
        d_naT = sem("d_naT")
        d_naT_copied = sem("d_naT_copied")
        d_adj = [sem(f"d_adj{b}") for b in range(2)]
        d_mask = sem("d_mask")
        d_xag = sem("d_xag")
        d_score = sem("d_score")
        d_neg = sem("d_neg")
        d_leaky = sem("d_leaky")
        d_rmax = sem("d_rmax")
        d_nmax = sem("d_nmax")
        d_exp = sem("d_exp")
        d_xpose = sem("d_xpose")
        d_pt = [sem(f"d_pt{k}") for k in range(2)]
        d_agg = sem("d_agg")
        d_rinv = sem("d_rinv")
        d_xres = sem("d_xres")
        d_right = sem("d_right")
        d_stored = sem("d_stored")

        pe_gate, dve_gate, pool_gate = sem("pe_gate"), sem("dve_gate"), sem("pool_gate")

        def ahead(g, r):
            return g + r // R, r % R

        def first(g, t, n):
            return isinstance(g, int) and t <= n

        block = ctx.enter_context(nc.Block())

        @block.sync
        def _(sp):
            def load(dst, src):
                sp.dma_start(dst, src).then_inc(weights_loaded, 16)

            for s, a, b_, c, d_ in (("n", Wn1, Wn2, Wv, bn1), ("x", Wx1, Wx2, Wfx, bx1)):
                load(w1[s][:], a.rearrange("(k p) h -> p k h", p=P))
                load(w2[s][:], b_)
                load(ww[s][:], c.rearrange("(k p) h -> p k h", p=P))
                load(b1[s][:], d_.rearrange("(h a) -> h a", a=1))
            load(b2x[:], bx2.rearrange("(h a) -> h a", a=1))
            load(b2n[:], bn2.partition_broadcast(P))
            load(bvb[:], bv.partition_broadcast(P))
            load(bfb[:], bfx.partition_broadcast(P))

            for r in range(R):
                sp.dma_start(adjt[r][:, :, 0:QW], adj_q[0, :, r]).then_inc(adj_loaded[r], 16)

            def adj_loads(g):
                for r in range(R):
                    t = R * g + r
                    sp.wait_ge(quarter_found, NQ * (t + 1))
                    sp.wait_ge(adj_summed, 2 * (t + 1) + 1)
                    sp.dma_start(adjt[r][:, :, 0:QW], adj_q[g + 1, :, r]).then_inc(adj_loaded[r], 16)

            with sp.Fori(0, 2) as g:
                adj_loads(g)
            with sp.Fori(0, G) as g:
                sp.dma_start(xright[:, bass.ds(R * g, R), :], x_v[g, :, :, DO:D]).then_inc(xright_loaded, 16)
            with sp.Fori(2, G - 1) as g:
                adj_loads(g)

            with sp.Fori(0, G) as g:
                sp.wait_ge(result_ready, R * (g + 1))
                sp.dma_start(out_v[g, :, :, DO:D], xright[:, bass.ds(R * g, R), :]).then_inc(result_stored, 16)
            sp.wait_ge(result_stored, 16 * G)

            sp.wait_ge(flag_ready, 1)
            incomplete = sp.value_load(flag[0:1, 0:1], min_val=0, max_val=1)
            with sp.If(incomplete != 0):
                for b in range(2):
                    sp.wait_ge(xs.stored[b], 16 * (G // 2 + 1))
                sp.dma_start(V[:], tab_r[:, :, 0:DO]).then_inc(d_table, 16)
                sp.dma_start(na, tab_r[:, :, DO:TW]).then_inc(d_table, 16)
                for r in range(2):
                    sp.dma_start(d_adjt[r], adj_v[0, :, r, :]).then_inc(d_adj[r], 16)

                def dense_loads(g, last):
                    sp.wait_ge(d_right, R * g + 1)
                    sp.dma_start(xres[:], x_v[g, :, :, DO:D]).then_inc(d_xres, 16)
                    for r in range(2, R):
                        sp.wait_ge(d_mask, R * g + r - 1)
                        sp.dma_start(d_adjt[r % 2], adj_v[g, :, r, :]).then_inc(d_adj[r % 2], 16)
                    for r in range(0 if last else 2):
                        sp.wait_ge(d_mask, R * g + r + 3)
                        sp.dma_start(d_adjt[r], adj_v[g + 1, :, r, :]).then_inc(d_adj[r], 16)

                with sp.Fori(0, G - 1) as g:
                    dense_loads(g, False)
                dense_loads(G - 1, True)

        @block.gpsimd
        def _(pool):
            for b in range(2):
                pool.dma_start(rows[b][:], n_v[b]).then_inc(nb.rows_loaded[b], 16)

            def fill(t, v):
                nc.gpsimd.memset(t, v).then_inc(filled, 1)
                nfilled[0] += 1

            nfilled = [0]
            for m in (ident, identb, nextdiff, maskdiff, maskrow, firstrow, quarter):
                fill(m[:], 0.0)
            fill(before[:], 1.0)
            fill(upto[:], 1.0)
            pool.wait_ge(filled, nfilled[0])

            def select(m, op, fill_, base, mult=1, step=-1, n=P):
                pool.wait_ge(filled, nfilled[0])
                nc.gpsimd.affine_select(out=m, in_=m, compare_op=op, fill=fill_, base=base,
                                        pattern=[[step, n]], channel_multiplier=mult).then_inc(filled, 1)
                nfilled[0] += 1

            select(ident[:], ALU.not_equal, 1.0, 0)
            select(identb[:], ALU.not_equal, 1.0, 0)
            select(before[:], ALU.is_ge, 0.0, -1, -1, 1)
            select(upto[:], ALU.is_ge, 0.0, 0, -1, 1)
            select(nextdiff[:], ALU.not_equal, -1.0, 0)
            select(nextdiff[:], ALU.not_equal, 1.0, -1)
            select(maskdiff[:], ALU.not_equal, -BIG, 0)
            select(maskdiff[:], ALU.not_equal, BIG, 1)
            select(maskrow[:], ALU.not_equal, -BIG, 0, 1, 0)
            select(firstrow[:], ALU.not_equal, 1.0, 0, 1, 0)
            for q in range(NQ):
                select(quarter[:, SS + 8 * q:SS + 8 * q + 8], ALU.not_equal, float(NONE - QW * q), 0, 1, 0, 8)
            select(quarter[:, SS + S:2 * SS], ALU.not_equal, float(NONE - M), 0, 1, 0, 1)
            pool.wait_ge(filled, nfilled[0])
            nc.gpsimd.memset(maskrow[:, 0:1], 0.0).then_inc(consts_ready, 1)
            nc.gpsimd.iota(colno[:], pattern=[[1, E]], base=0, channel_multiplier=0,
                           allow_small_or_imprecise_dtypes=True).then_inc(consts_ready, 1)
            nc.gpsimd.iota(colid[:], pattern=[[P, C]], base=1, channel_multiplier=1,
                           allow_small_or_imprecise_dtypes=True).then_inc(consts_ready, 1)
            nc.gpsimd.memset(halfneg[:], -0.5).then_inc(consts_ready, 1)
            nc.gpsimd.memset(vsum[:], 0.0).then_inc(consts_ready, 1)
            nc.gpsimd.memset(vmean[:], 0.0).then_inc(consts_ready, 1)
            for r in range(R):
                nc.gpsimd.memset(cols[r][:], 0.0).then_inc(consts_ready, 1)
            pool.wait_ge(consts_ready, 6 + R)

            def neigh_group(j, b, src, loaded):
                pool.wait_ge(nb.transposed, 2 * (j + 1))
                pool.dma_start(rows[b][:], src).then_inc(loaded, 16)
                pool.wait_ge(nb.wide_copied, j + 2)
                pool.wait_ge(vsum_added, j + 2)
                nc.gpsimd.tensor_tensor(vsum[:], vsum[:], tab[b][:, :, 0:DO], ALU.add).then_inc(vsum_added, 1)

            with pool.Fori(0, G // 2 - 1) as it:
                for b in range(2):
                    neigh_group(2 * it + b, b, n_v[2 * it + 2 + b], nb.rows_loaded[b])
            for b in range(2):
                neigh_group(G - 2 + b, b, x_v[b], xs.rows_loaded[b])
            pool.wait_ge(weights_loaded, 16 * NWL)

            def x_group(j, b, it):
                pool.wait_ge(var_ready, R * (j + 1))
                pool.wait_ge(shift_ready, j + 1)
                pool.sem_inc(pool_gate, 1)
                nc.gpsimd.tensor_scalar(vareps[:], meanvar[:, :, 1], EPS, None, ALU.add).then_inc(vareps_ready, 1)
                pool.wait_ge(vareps_ready, j + 1)
                pool.wait_ge(h_ready, R * j + 1)
                nc.gpsimd.tensor_tensor(rstd[:], vareps[:], halfneg[:], ALU.pow).then_inc(rstd_ready, 1)
                pool.wait_ge(xs.rows_loaded[b], 16 * (it + 1))
                pool.wait_ge(xs.wide_copied, j + 1)
                nc.gpsimd.tensor_tensor(xbias[:], rows[b][:, :, 0:DO],
                                        bfb[:].unsqueeze(1).to_broadcast([P, R, DO]),
                                        ALU.add).then_inc(xbias_ready, 1)

            with pool.Fori(0, G // 2 - 1) as it:
                for b in range(2):
                    x_group(2 * it + b, b, it)
                    pool.wait_ge(xbias_ready, 2 * it + b + 1)
                    pool.wait_ge(h_ready, R * (2 * it + b + 1) + 1)
                    pool.dma_start(rows[b][:], x_v[2 * it + 2 + b]).then_inc(xs.rows_loaded[b], 16)
            for b in range(2):
                x_group(G - 2 + b, b, G // 2 - 1)

            def gather(g, r):
                t = R * g + r
                if not first(g, t, 3):
                    pool.wait_ge(scored, t - 3)
                pool.wait_ge(xs.second_copied, G + 1)
                nc.gpsimd.tensor_copy(xat[r][:], xaT[:, bass.ds(t * P, P)]).then_inc(xat_ready, 1)
                pool.wait_ge(index_ready, t + 1)
                if not first(g, t, 3):
                    pool.wait_ge(summed_up, t - 3)
                pool.sem_inc(pool_gate, 1)
                for c in range(C):
                    nc.gpsimd.indirect_dma_start(cols[r][:, c, :], None, table[:, :],
                                                 bass.IndirectOffsetOnAxis(ap=index[r][:, c:c + 1], axis=0),
                                                 bounds_check=M, oob_is_err=False).then_inc(gathered[r], 16)

            for b in range(2):
                pool.wait_ge(nb.stored[b], 16 * (G // 2 + 1))
            pool.wait_ge(mean_stored, 16)
            for r in range(R):
                gather(0, r)
            with pool.Fori(1, G) as g:
                for r in range(R):
                    gather(g, r)

        @block.tensor
        def _(pe):
            def transposes(sd, j, src):
                for k, copied in enumerate((sd.T0_copied, sd.T1_copied)):
                    pe.wait_ge(copied, j + 1)
                    for r in range(R):
                        last = nc.tensor.transpose(psT[k][:, r * P:(r + 1) * P], src[:, r, k * P:(k + 1) * P], ident[:])
                    last.then_inc(sd.transposed, 1)

            def hidden(sd, j, b):
                pe.wait_ge(sd.T0_copied, j + 2)
                pe.wait_ge(sd.T1_copied, j + 2)
                pe.wait_ge(sd.tanh_ready, j + 1)
                for k in range(KD):
                    last = nc.tensor.matmul(psH[0:H, :], w1[sd.name][:, k, :], rowsT[b][:, k, :],
                                            start=k == 0, stop=k == KD - 1)
                last.then_inc(sd.hidden, 1)

            def wide(sd, j, b):
                pe.wait_ge(sd.wide_copied, j + 1)
                for r in range(R):
                    for k in range(KD):
                        last = nc.tensor.matmul(psW[b][:, r * DO:(r + 1) * DO], rowsT[b][:, k, r * P:(r + 1) * P],
                                                ww[sd.name][:, k, :], start=k == 0, stop=k == KD - 1)
                last.then_inc(sd.wide, 1)

            def second_n(j, b):
                pe.wait_ge(nb.tanh_ready, j + 2)
                pe.wait_ge(nb.second_copied, j + 1)
                pe.sem_inc(pe_gate, 1)
                for r in range(R):
                    last = nc.tensor.matmul(psS[b][:, r * H:(r + 1) * H], tanhT[:, r * P:(r + 1) * P], w2["n"][:],
                                            start=True, stop=True)
                last.then_inc(nb.second, 1)

            def second_x(j, b):
                pe.wait_ge(xs.tanh_ready, j + 2)
                pe.wait_ge(xs.second_copied, j + 1)
                pe.sem_inc(pe_gate, 1)
                nc.tensor.matmul(psS[b][0:H, :], w2["x"][:], tanhT[:], start=True, stop=True).then_inc(xs.second, 1)

            pe.wait_ge(consts_ready, 1)
            pe.wait_ge(weights_loaded, 16 * NWL)
            pe.wait_ge(nb.rows_loaded[0], 16)
            transposes(nb, 0, rows[0])

            def neigh_group(j, b, nxt, last):
                hidden(nb, j, b)
                if not last:
                    pe.wait_ge(nb.rows_loaded[1 - b], nxt)
                    transposes(nb, j + 1, rows[1 - b])
                wide(nb, j, b)
                second_n(j, b)

            with pe.Fori(0, G // 2 - 1) as it:
                for b in range(2):
                    neigh_group(2 * it + b, b, 16 * (it + 1 + b), False)
            for b in range(2):
                neigh_group(G - 2 + b, b, 16 * (G // 2), b == 1)

            pe.wait_ge(vsum_added, G + 2)
            pe.wait_ge(vec_consts, NVC)
            for r in range(R):
                last = nc.tensor.matmul(psMean, meanw[:], vsum[:, r, :], start=r == 0, stop=r == R - 1)
            last.then_inc(mean_ready, 1)

            pe.wait_ge(nb.wide_copied, G + 1)
            pe.wait_ge(nb.second_copied, G + 1)
            pe.wait_ge(h_ready, R + 1)
            pe.wait_ge(vmean_copied, 1)
            transposes(xs, 0, hgrp)

            def x_group(j, b, last):
                hidden(xs, j, b)
                if not last:
                    pe.wait_ge(h_ready, R * (j + 2) + 1)
                    transposes(xs, j + 1, hgrp)
                wide(xs, j, b)
                second_x(j, b)

            with pe.Fori(0, G // 2 - 1) as it:
                for b in range(2):
                    x_group(2 * it + b, b, False)
            for b in range(2):
                x_group(G - 2 + b, b, b == 1)
            pe.wait_ge(xs.wide_copied, G + 1)
            pe.wait_ge(xs.second_copied, G + 1)

            def ends(g, r):
                t = R * g + r
                pe.wait_ge(total_ready, t + 1)
                pe.wait_ge(hit_ready, t + 1)
                nc.tensor.matmul(psStart, before[:], total[r % 2][:], start=True, stop=True)
                nc.tensor.matmul(psEnd, upto[:], total[r % 2][:], start=True, stop=True).then_inc(ends_ready, 1)

            def diff(g, r):
                t = R * g + r
                pe.wait_ge(places_ready, t + 1)
                pe.wait_ge(passed_ready, t + 2)
                nc.tensor.matmul(psDiff, nextdiff[:], places[:, t, :], start=True, stop=True).then_inc(diff_made, 1)

            def pick(g, r):
                t = R * g + r
                pe.wait_ge(diffs_copied, t + 2)
                for c in range(C):
                    nc.tensor.matmul(psPick[:, c, :], passed[r][:, c * P:(c + 1) * P], diffs[:], start=True, stop=False)
                    nc.tensor.matmul(psPick[:, c, :], firstrow[:], places[:, t, :], start=False, stop=False)
                    last = nc.tensor.matmul(psPick[:, c, :], firstrow[:], quarter[:], start=False, stop=True)
                last.then_inc(picked, 1)

            def turn_cols(g, r):
                t = R * g + r
                pe.wait_ge(gathered[r], 16 * C * (g + 1))
                pe.wait_ge(colsT_copied, t + 1)
                for c in range(C):
                    last = nc.tensor.transpose(bankA[0:H, c * P:(c + 1) * P], cols[r][:, c, DO:TW], ident[:])
                last.then_inc(colsT_made, 1)

            def scores(g, r):
                t = R * g + r
                pe.wait_ge(colsT_copied, t + 2)
                pe.wait_ge(xat_ready, t + 1)
                pe.wait_ge(leaky_ready, t + 1)
                for a, b in ((0, 512), (512, E)):
                    nc.tensor.matmul(psScore[:, a:b], maskrow[:], onesb[:, 0:b - a], start=True, stop=False)
                    nc.tensor.matmul(psScore[:, a:b], maskdiff[:], passed[r][:, a:b], start=False, stop=False)
                    last = nc.tensor.matmul(psScore[:, a:b], xat[r][:], colsT[:, a:b], start=False, stop=True)
                last.then_inc(scored, 1)

            def turn_probs(g, r):
                t = R * g + r
                pe.wait_ge(exp_ready, t + 1)
                pe.wait_ge(probT_copied, t + 1)
                for c in range(C):
                    last = nc.tensor.transpose(psProbT[:, c * P:(c + 1) * P], prob[r % 2][:, c * P:(c + 1) * P], ident[:])
                last.then_inc(probT_made, 1)

            def mix(g, r):
                t = R * g + r
                pe.wait_ge(probT_copied, t + 2)
                if not first(g, t, 0):
                    pe.wait_ge(result_ready, t)
                for c in range(C):
                    last = nc.tensor.matmul(psOut, probT[:, c * P:(c + 1) * P], cols[r][:, c, 0:DO],
                                            start=c == 0, stop=c == C - 1)
                last.then_inc(summed_up, 1)

            def lists(g, r):
                ends(g, r)
                diff(g, r)
                pick(g, r)

            for r in range(3):
                lists(0, r)
            turn_cols(0, 0)
            scores(0, 0)

            def step(g, r, to_list, to_score):
                g3, r3 = ahead(g, r + 3)
                g1, r1 = ahead(g, r + 1)
                if to_list:
                    ends(g3, r3)
                if to_score:
                    turn_cols(g1, r1)
                if to_list:
                    diff(g3, r3)
                turn_probs(g, r)
                if to_list:
                    pick(g3, r3)
                if to_score:
                    scores(g1, r1)
                mix(g, r)

            for r in range(R):
                step(0, r, True, True)
            with pe.Fori(1, G // 2) as g:
                for r in range(R):
                    step(g, r, True, True)
            pe.wait_ge(result_ready, NT // 2)
            pe.wait_ge(check_step, 3)
            nc.tensor.matmul(psCheck, onesf[:], slots[:], start=True, stop=True).then_inc(check_sum, 1)
            pe.wait_ge(check_step, 6)
            nc.tensor.matmul(psCheck[:, 0:1], onesf[:], badsum[:], start=True, stop=True).then_inc(check_sum, 1)
            pe.wait_ge(flag_ready, 1)
            with pe.Fori(G // 2, G - 1) as g:
                for r in range(R):
                    step(g, r, True, True)
            for r in range(R):
                step(G - 1, r, r == 0, r < R - 1)

            pe.wait_ge(flag_ready, 1)
            incomplete = pe.value_load(flag[0:1, 0:1], min_val=0, max_val=1)
            with pe.If(incomplete != 0):
                pe.wait_ge(result_ready, NT)
                pe.wait_ge(d_table, 32)
                for q in range(Q):
                    if q >= 2:
                        pe.wait_ge(d_naT_copied, q - 1)
                    for c in range(4):
                        last = nc.tensor.transpose(dbank[q % 2][0:H, c * P:(c + 1) * P], na[:, 4 * q + c, :], ident[:])
                    last.then_inc(d_naT, 1)
                pe.wait_ge(d_naT_copied, Q)
                with pe.Fori(0, G) as g:
                    pe.wait_ge(d_xag, g + 1)
                    for r in range(R):
                        t = R * g + r
                        pe.wait_ge(d_mask, t + 1)
                        for q in range(Q):
                            pe.wait_ge(d_leaky, Q * t + q + 1)
                            nc.tensor.matmul(dbank[q % 2], identb[:], masked[:, q * 512:(q + 1) * 512], start=True, stop=False)
                            nc.tensor.matmul(dbank[q % 2], xag[:, r * P:(r + 1) * P], naT[:, q * 512:(q + 1) * 512],
                                             start=False, stop=True).then_inc(d_score, 1)

                        def weights_T(u):
                            pe.wait_ge(d_pt[u % 2], (Q // 2) * t + u // 2 + 1)
                            for c in range(4):
                                last = nc.tensor.transpose(dbank[2 + u % 2][:, c * P:(c + 1) * P],
                                                           L[:, (4 * u + c) * P:(4 * u + c + 1) * P], ident[:])
                            last.then_inc(d_xpose, 1)

                        pe.wait_ge(d_exp, t + 1)
                        pe.wait_ge(d_right, t + 1)
                        weights_T(0)
                        for u in range(Q):
                            if u + 1 < Q:
                                weights_T(u + 1)
                            pe.wait_ge(d_pt[u % 2], (Q // 2) * t + u // 2 + 2)
                            for c in range(4):
                                last = nc.tensor.matmul(dbank[4][:, 0:DO], PT[u % 2][:, c * P:(c + 1) * P], V[:, 4 * u + c, :],
                                                        start=(u == 0 and c == 0), stop=(u == Q - 1 and c == 3))
                        last.then_inc(d_agg, 1)

        @block.scalar
        def _(act):
            for s in (nb.T0_copied, nb.tanh_ready, xs.T0_copied, xs.tanh_ready, xs.second_copied, h_ready,
                      diffs_copied, colsT_copied, probT_copied):
                act.sem_inc(s, 1)
            for b in range(2):
                act.sem_inc(nb.stored[b], 16)
                act.sem_inc(xs.stored[b], 16)
            act.wait_ge(weights_loaded, 16 * NWL)

            def add_up(g, r, half):
                if half == 0:
                    act.wait_ge(adj_loaded[r], 16 * (g + 1))
                act.wait_ge(adj_summed, 2 * (R * g + r) + half + 1)
                nc.scalar.activation(sink[:], adjt[r][:, 2 * half:2 * half + 2, 0:QW], ACT.Relu,
                                     accum_out=adjsum[:, R * g + r, half:half + 1]).then_inc(adj_summed, 1)

            with act.Fori(0, 2) as it:
                for r in range(R):
                    j, b = R * it + r, r % 2
                    act.wait_ge(nb.transposed, 2 * j + 1)
                    nc.scalar.activation(rowsT[b][:, 0, :], psT[0], ACT.Copy).then_inc(nb.T0_copied, 1)
                    add_up(it, r, 0)
                    act.wait_ge(nb.hidden, j + 1)
                    nc.scalar.activation(tanhT[:], psH[0:H, :], ACT.Tanh, bias=b1["n"][:]).then_inc(nb.tanh_ready, 1)
                    add_up(it, r, 1)
                    act.wait_ge(nb.second_copied, j + 2)
                    act.wait_ge(nb.wide_copied, j + 2)
                    act.dma_start(tab_w[j], tab[b][:]).then_inc(nb.stored[b], 16)
            act.wait_ge(mean_ready, 1)
            act.wait_ge(consts_ready, 6 + R)
            nc.scalar.activation(vmean[:, 0:DO], psMean, ACT.Copy).then_inc(vmean_copied, 1)
            act.wait_ge(vmean_copied, 1)
            act.dma_start(table[M:M + 1, :], vmean[:]).then_inc(mean_stored, 16)

            def normalise(j):
                act.wait_ge(shift_ready, j + 2)
                for i in range(R):
                    nc.scalar.activation(hgrp[:, i, :], rows[j % 2][:, i, :], ACT.Relu, scale=rstd[:, i:i + 1],
                                         bias=shift[:, i:i + 1]).then_inc(h_ready, 1)

            def x_groups(it):
                for r in range(R):
                    j, b = R * it + r, r % 2
                    act.wait_ge(xs.transposed, 2 * j + 1)
                    nc.scalar.activation(rowsT[b][:, 0, :], psT[0], ACT.Copy).then_inc(xs.T0_copied, 1)
                    if j + 1 < G:
                        act.wait_ge(xs.transposed, 2 * j + 2)
                        normalise(j + 1)
                    add_up(it + 2, r, 0)
                    act.wait_ge(xs.hidden, j + 1)
                    nc.scalar.activation(tanhT[:], psH[0:H, :], ACT.Tanh, bias=b1["x"][:]).then_inc(xs.tanh_ready, 1)
                    add_up(it + 2, r, 1)
                    act.wait_ge(xs.second, j + 1)
                    nc.scalar.activation(xaT[:, bass.ds(j * GW, GW)], psS[b][0:H, :], ACT.Identity,
                                         bias=b2x[:]).then_inc(xs.second_copied, 1)
                    act.wait_ge(xs.wide_copied, j + 2)
                    act.dma_start(out_v[j, :, :, 0:DO], left[b][:]).then_inc(xs.stored[b], 16)

            normalise(0)
            for it in range(2):
                x_groups(it)
            for b in range(2):
                act.wait_ge(xs.stored[b], 16 * (G // 2 + 1))

            def copy_diffs(g, r):
                t = R * g + r
                act.wait_ge(diff_made, t + 1)
                if not first(g, t, 0):
                    act.wait_ge(picked, t)
                nc.scalar.activation(diffs[:], psDiff, ACT.Copy).then_inc(diffs_copied, 1)

            def copy_colsT(g, r):
                t = R * g + r
                act.wait_ge(colsT_made, t + 1)
                if not first(g, t, 0):
                    act.wait_ge(scored, t)
                nc.scalar.activation(colsT[:], psColsT, ACT.Copy).then_inc(colsT_copied, 1)

            def negative_part(g, r):
                t = R * g + r
                act.wait_ge(scored, t + 1)
                act.wait_ge(leaky_ready, t + 1)
                nc.scalar.activation(neg[:], psScore, ACT.Relu, scale=-0.99).then_inc(neg_ready, 1)

            def exponentials(g, r):
                t = R * g + r
                act.wait_ge(nmax_ready, t + 1)
                if not first(g, t, 1):
                    act.wait_ge(sinv_ready, t - 1)
                nc.scalar.activation(prob[r % 2][:], prob[r % 2][:], ACT.Exp, bias=snmax[r % 2][:],
                                     accum_out=ssum[r % 2][:]).then_inc(exp_ready, 1)

            def copy_probT(g, r):
                t = R * g + r
                act.wait_ge(probT_made, t + 1)
                if not first(g, t, 0):
                    act.wait_ge(summed_up, t)
                nc.scalar.activation(probT[:], psProbT, ACT.Copy).then_inc(probT_copied, 1)

            for r in range(3):
                copy_diffs(0, r)
            copy_colsT(0, 0)
            negative_part(0, 0)

            def step(g, r, to_add, to_list, to_score):
                g3, r3 = ahead(g, r + 3)
                g1, r1 = ahead(g, r + 1)
                exponentials(g, r)
                if to_add:
                    add_up(g + G // 2, r, 0)
                if to_list:
                    copy_diffs(g3, r3)
                if to_score:
                    copy_colsT(g1, r1)
                copy_probT(g, r)
                if to_add:
                    add_up(g + G // 2, r, 1)
                if to_score:
                    negative_part(g1, r1)

            for r in range(R):
                step(0, r, True, True, True)
            with act.Fori(1, G // 2) as g:
                for r in range(R):
                    step(g, r, True, True, True)
            with act.Fori(G // 2, G - 1) as g:
                for r in range(R):
                    step(g, r, False, True, True)
            for r in range(R):
                step(G - 1, r, False, r == 0, r < R - 1)

            act.wait_ge(flag_ready, 1)
            incomplete = act.value_load(flag[0:1, 0:1], min_val=0, max_val=1)
            with act.If(incomplete != 0):
                act.sem_inc(d_pt[0], 1)
                act.sem_inc(d_stored, 16)
                with act.Fori(0, G) as g:
                    nc.scalar.activation(xag[:], xaT[:, bass.ds(g * GW, GW)], ACT.Copy).then_inc(d_xag, 1)
                    for r in range(R):
                        t = R * g + r
                        for q in range(Q):
                            act.wait_ge(d_score, Q * t + q + 1)
                            act.wait_ge(d_leaky, Q * t + q + 1)
                            nc.scalar.activation(negpart[q % 2], dbank[q % 2], ACT.Relu, scale=-0.99).then_inc(d_neg, 1)
                        act.wait_ge(d_nmax, t + 1)
                        act.wait_ge(d_rinv, t + 1)
                        nc.scalar.activation(L, L, ACT.Exp, bias=nmax[:], accum_out=rsum[:]).then_inc(d_exp, 1)
                        for u in range(0, Q, 2):
                            act.wait_ge(d_xpose, Q * t + u + 1)
                            nc.scalar.activation(PT[0], dbank[2], ACT.Copy).then_inc(d_pt[0], 1)
                    act.wait_ge(d_right, R * (g + 1) + 1)
                    act.wait_ge(result_stored, 16 * G)
                    act.dma_start(out_v[g, :, :, DO:D], right[:]).then_inc(d_stored, 16)
                act.wait_ge(d_stored, 16 * (G + 1))

        @block.vector
        def _(dve):
            for s in (nb.T1_copied, nb.wide_copied, nb.second_copied, xs.T1_copied, xs.wide_copied, shift_ready,
                      passed_ready, hit_ready, leaky_ready, adj_summed):
                dve.sem_inc(s, 1)
            dve.sem_inc(vsum_added, 2)
            for t, v in [(ones_i[:], 1), (onesS[:], 1.0), (onesb[:], 1.0), (onesf[:], 1.0), (meanw[:], 1.0 / M),
                         (places[:, :, SS + S:2 * SS], 0.0)] + [(adjt[r][:, :, QW:QP], 1) for r in range(R)]:
                nc.vector.memset(t, v).then_inc(vec_consts, 1)
            dve.wait_ge(vec_consts, NVC)
            dve.wait_ge(weights_loaded, 16 * NWL)
            dve.wait_ge(consts_ready, 6 + R)

            def find(g, r, q):
                if q == 0:
                    dve.wait_ge(adj_loaded[r], 16 * (g + 1))
                    dve.sem_inc(dve_gate, 1)
                nc.vector.max_index(found[r % 2][:, 8 * q:8 * q + 8], ones_i[:], adjt[r][:, q, :]).then_inc(quarter_found, 1)

            def keep(g, r):
                t = R * g + r
                dve.wait_ge(quarter_found, NQ * (t + 1))
                nc.vector.tensor_scalar(valid[:, t, 0:S], found[r % 2][:], float(QW), None, ALU.is_lt).then_inc(valid_ready, 1)
                nc.vector.tensor_scalar(places[:, t, SS:SS + S], found[r % 2][:], -1.0, None, ALU.mult).then_inc(value_ready, 1)

            with dve.Fori(0, 2) as it:
                for r in range(R):
                    j, b = R * it + r, r % 2
                    find(it, r, 0)
                    dve.wait_ge(nb.transposed, 2 * j + 2)
                    nc.vector.tensor_copy(rowsT[b][:, 1, :], psT[1]).then_inc(nb.T1_copied, 1)
                    find(it, r, 1)
                    find(it, r, 2)
                    dve.wait_ge(nb.wide, j + 1)
                    dve.wait_ge(nb.stored[b], 16 * (2 * it + r // 2 + 1))
                    dve.wait_ge(vsum_added, j + 1)
                    nc.vector.tensor_tensor(tab[b][:, :, 0:DO], psW[b].rearrange("p (r d) -> p r d", r=R),
                                            bvb[:].unsqueeze(1).to_broadcast([P, R, DO]), ALU.add).then_inc(nb.wide_copied, 1)
                    find(it, r, 3)
                    keep(it, r)
                    dve.wait_ge(nb.second, j + 1)
                    nc.vector.tensor_tensor(tab[b][:, :, DO:TW], psS[b][:, 0:R * H].rearrange("p (r d) -> p r d", r=R),
                                            b2n[:].unsqueeze(1).to_broadcast([P, R, H]), ALU.add).then_inc(nb.second_copied, 1)
            def moments(j):
                dve.wait_ge(xs.rows_loaded[j % 2], 16 * (j // 2 + 1))
                for i in range(R):
                    nc.vector.bn_stats(stats[:, i, :], rows[j % 2][:, i, :]).then_inc(stats_ready, 1)
                dve.wait_ge(stats_ready, R * (j + 1))
                for i in range(R):
                    nc.vector.bn_aggr(meanvar[:, i, :], stats[:, i, :]).then_inc(var_ready, 1)

            def shifts(j):
                dve.wait_ge(rstd_ready, j + 1)
                dve.wait_ge(var_ready, R * (j + 1))
                nc.vector.scalar_tensor_tensor(shift[:], meanvar[:, :, 0], -1.0, rstd[:], ALU.mult,
                                               ALU.mult).then_inc(shift_ready, 1)

            def x_groups(it):
                for r in range(R):
                    j, b = R * it + r, r % 2
                    if j + 1 < G:
                        moments(j + 1)
                    dve.wait_ge(xs.transposed, 2 * j + 2)
                    nc.vector.tensor_copy(rowsT[b][:, 1, :], psT[1]).then_inc(xs.T1_copied, 1)
                    find(it + 2, r, 0)
                    if j + 1 < G:
                        shifts(j + 1)
                    find(it + 2, r, 1)
                    find(it + 2, r, 2)
                    find(it + 2, r, 3)
                    keep(it + 2, r)
                    dve.wait_ge(xs.wide, j + 1)
                    dve.wait_ge(xbias_ready, j + 1)
                    dve.wait_ge(xs.stored[b], 16 * (j // 2 + 1))
                    nc.vector.tensor_tensor(left[b][:], psW[b].rearrange("p (r d) -> p r d", r=R), xbias[:],
                                            ALU.add).then_inc(xs.wide_copied, 1)

            moments(0)
            shifts(0)
            for it in range(2):
                x_groups(it)

            def count(g, r):
                t = R * g + r
                b = r % 2
                dve.wait_ge(valid_ready, t + 1)
                nc.vector.tensor_tensor_scan(cum[b][:, 0:S], onesS[:], valid[:, t, 0:S], 0.0, ALU.mult,
                                             ALU.add).then_inc(scanned, 1)
                dve.wait_ge(scanned, t + 1)
                nc.vector.tensor_scalar(total[b][:], cum[b][:, S - 1:S], 1.0, None, ALU.max).then_inc(total_ready, 1)
                nc.vector.tensor_scalar(cum[b][:, S:SS], cum[b][:, S - 1:S], 1.0, None, ALU.max).then_inc(spare_cum, 1)
                nc.vector.tensor_scalar(valid[:, t, S:SS], cum[b][:, S - 1:S], 0.0, None, ALU.is_equal).then_inc(spare_valid, 1)

            def place(g, r):
                t = R * g + r
                b = r % 2
                dve.wait_ge(ends_ready, t + 1)
                dve.wait_ge(spare_cum, t + 1)
                dve.wait_ge(spare_valid, t + 1)
                nc.vector.scalar_tensor_tensor(places[:, t, 0:SS], cum[b][:], psStart, valid[:, t, :], ALU.add,
                                               ALU.mult).then_inc(places_ready, 1)
                if not first(g, t, 3):
                    dve.wait_ge(scored, t - 3)
                nc.vector.tensor_scalar(passed[r][:], colno[:], psEnd, None, ALU.is_ge).then_inc(passed_ready, 1)

            def list_up(g, r):
                t = R * g + r
                dve.wait_ge(picked, t + 1)
                nc.vector.tensor_tensor(match[:], psPick[:, :, 0:SS], colid[:].unsqueeze(2).to_broadcast([P, C, SS]),
                                        ALU.is_equal).then_inc(matched, 1)
                dve.wait_ge(matched, t + 1)
                nc.vector.tensor_tensor(hit[:], match[:], psPick[:, :, SS:2 * SS], ALU.mult).then_inc(hit_ready, 1)
                dve.wait_ge(hit_ready, t + 2)
                nc.vector.tensor_reduce(hitsum[:], hit[:], AX.X, ALU.add).then_inc(hits_summed, 1)
                dve.wait_ge(hits_summed, t + 1)
                if not first(g, t, 3):
                    dve.wait_ge(gathered[r], 16 * C * g)
                nc.vector.tensor_scalar(index[r][:], hitsum[:], -1.0, float(NONE), ALU.mult, ALU.add).then_inc(index_ready, 1)

            def leaky(g, r):
                t = R * g + r
                b = r % 2
                dve.wait_ge(neg_ready, t + 1)
                if not first(g, t, 1):
                    dve.wait_ge(probT_made, t - 1)
                dve.sem_inc(dve_gate, 1)
                nc.vector.tensor_tensor_reduce(out=prob[b][:], in0=psScore, in1=neg[:], scale=1.0, scalar=-3.0e38,
                                               op0=ALU.add, op1=ALU.max, accum_out=smax[b][:]).then_inc(leaky_ready, 1)
                dve.wait_ge(leaky_ready, t + 2)
                nc.vector.tensor_scalar(snmax[b][:], smax[b][:], -1.0, None, ALU.mult).then_inc(nmax_ready, 1)

            def invert(g, r):
                t = R * g + r
                dve.wait_ge(exp_ready, t + 1)
                nc.vector.reciprocal(sinv[:], ssum[r % 2][:]).then_inc(sinv_ready, 1)

            def result(g, r):
                t = R * g + r
                dve.wait_ge(sinv_ready, t + 1)
                dve.wait_ge(summed_up, t + 1)
                nc.vector.scalar_tensor_tensor(xright[:, t, :], psOut, sinv[:], xright[:, t, :], ALU.mult,
                                               ALU.add).then_inc(result_ready, 1)

            for r in range(3):
                count(0, r)
                place(0, r)
                list_up(0, r)
            dve.wait_ge(xright_loaded, 16 * G)

            def step(g, r, to_find, to_list):
                g3, r3 = ahead(g, r + 3)
                z = g + G // 2
                leaky(g, r)
                if to_list:
                    count(g3, r3)
                if to_find:
                    find(z, r, 0)
                if to_list:
                    place(g3, r3)
                if to_find:
                    find(z, r, 1)
                    find(z, r, 2)
                if to_list:
                    list_up(g3, r3)
                if to_find:
                    find(z, r, 3)
                    keep(z, r)
                invert(g, r)
                result(g, r)

            for r in range(R):
                step(0, r, True, True)
            with dve.Fori(1, G // 2) as g:
                for r in range(R):
                    step(g, r, True, True)

            dve.wait_ge(valid_ready, NT)
            nc.vector.tensor_reduce(counts[:], valid[:, :, 0:S], AX.X, ALU.add).then_inc(check_step, 1)
            dve.wait_ge(adj_summed, 2 * NT + 1)
            nc.vector.tensor_tensor(sums[:], adjsum[:, :, 0], adjsum[:, :, 1], ALU.add).then_inc(check_step, 1)
            dve.wait_ge(check_step, 2)
            nc.vector.tensor_scalar(slots[:], counts[:], 1.0, None, ALU.max).then_inc(check_step, 1)
            nc.vector.tensor_tensor(bad[:, 0, :], sums[:], counts[:], ALU.not_equal).then_inc(check_step, 1)
            dve.wait_ge(check_sum, 1)
            nc.vector.tensor_scalar(bad[:, 1, :], psCheck, float(E), None, ALU.is_gt).then_inc(check_step, 1)
            dve.wait_ge(check_step, 5)
            nc.vector.tensor_reduce(badsum[:], bad[:], AX.XY, ALU.add).then_inc(check_step, 1)
            dve.wait_ge(check_sum, 2)
            nc.vector.tensor_scalar(flag[:], psCheck[0:1, 0:1], 0.0, None, ALU.is_gt).then_inc(flag_ready, 1)

            with dve.Fori(G // 2, G - 1) as g:
                for r in range(R):
                    step(g, r, False, True)
            for r in range(R):
                step(G - 1, r, False, r == 0)

            dve.wait_ge(flag_ready, 1)
            incomplete = dve.value_load(flag[0:1, 0:1], min_val=0, max_val=1)
            with dve.If(incomplete != 0):
                dve.sem_inc(d_leaky, 2)
                dve.sem_inc(d_pt[1], 1)
                dve.sem_inc(d_right, 1)
                dve.sem_inc(d_rinv, 1)
                for q in range(Q):
                    dve.wait_ge(d_naT, q + 1)
                    nc.vector.tensor_copy(naT[:, q * 512:(q + 1) * 512], dbank[q % 2][0:H, :]).then_inc(d_naT_copied, 1)
                with dve.Fori(0, G) as g:
                    for r in range(R):
                        t = R * g + r
                        dve.wait_ge(d_adj[r % 2], 32 * g + 16 * (r // 2) + 16)
                        nc.vector.tensor_scalar(masked, d_adjt[r % 2], 0.0, -BIG, ALU.is_le, ALU.mult).then_inc(d_mask, 1)
                        for q in range(Q):
                            dve.wait_ge(d_neg, Q * t + q + 1)
                            dve.sem_inc(dve_gate, 1)
                            nc.vector.tensor_tensor_reduce(out=L[:, q * 512:(q + 1) * 512], in0=dbank[q % 2],
                                                           in1=negpart[q % 2], scale=1.0, scalar=-3.0e38,
                                                           op0=ALU.add, op1=ALU.max,
                                                           accum_out=cmax[:, q:q + 1]).then_inc(d_leaky, 1)
                        dve.wait_ge(d_leaky, Q * (t + 1) + 2)
                        nc.vector.tensor_reduce(rmax[:], cmax[:], AX.X, ALU.max).then_inc(d_rmax, 1)
                        dve.wait_ge(d_rmax, t + 1)
                        nc.vector.tensor_scalar(nmax[:], rmax[:], -1.0, None, ALU.mult).then_inc(d_nmax, 1)
                        for u in range(1, Q, 2):
                            dve.wait_ge(d_xpose, Q * t + u + 1)
                            nc.vector.tensor_copy(PT[1], dbank[3]).then_inc(d_pt[1], 1)
                        dve.wait_ge(d_exp, t + 1)
                        nc.vector.reciprocal(rinv[:], rsum[:]).then_inc(d_rinv, 1)
                        dve.wait_ge(d_agg, t + 1)
                        dve.wait_ge(d_rinv, t + 2)
                        if r == 0:
                            dve.wait_ge(d_xres, 16 * (g + 1))
                            dve.wait_ge(d_stored, 16 * (g + 1))
                        nc.vector.scalar_tensor_tensor(right[:, r, :], dbank[4][:, 0:DO], rinv[:], xres[:, r, :],
                                                       ALU.mult, ALU.add).then_inc(d_right, 1)


_INS = ["x", "adj"] + ["L0_gnn_" + n for n in
        ("neigh", "Wx1", "bx1", "Wx2", "bx2", "Wn1", "bn1", "Wn2", "bn2", "Wv", "bv", "Wfx", "bfx")]


def kernel(**inputs):
    import numpy as np
    import concourse.bacc as bacc
    from concourse.bass_utils import run_bass_kernel_spmd

    nc = bacc.Bacc("TRN2", target_bir_lowering=False, num_devices=1)
    arrays, args = {}, []
    for name in _INS:
        a = np.ascontiguousarray(inputs[name])
        arrays[name] = a
        args.append(nc.dram_tensor(name, a.shape, mybir.dt.from_np(a.dtype), kind="ExternalInput").ap())
    args.append(nc.dram_tensor("out", arrays["x"].shape, mybir.dt.float32, kind="ExternalOutput").ap())
    preln_gnn(nc, *args)
    return run_bass_kernel_spmd(nc, [arrays], core_ids=[0]).results[0]["out"]
```

```python
import concourse.bass as bass
from concourse import mybir
from contextlib import ExitStack


def preln_gnn(nc, x, adj, neigh, Wx1, bx1, Wx2, bx2, Wn1, bn1, Wn2, bn2, Wv, bv, Wfx, bfx, out):
    f32, bf16, f16, i32, u32 = (mybir.dt.float32, mybir.dt.bfloat16, mybir.dt.float16, mybir.dt.int32,
                                mybir.dt.uint32)
    ALU = mybir.AluOpType
    ACT = mybir.ActivationFunctionType
    AX = mybir.AxisListType

    P = 128
    N, D = x.shape
    M = neigh.shape[0]
    H = Wx1.shape[1]
    DO = Wv.shape[1]
    KD = D // P
    R = 4
    G = N // (P * R)
    NT = N // P
    GW = P * R
    TW = DO + H
    MC = M // P
    Q = M // 512
    BIG = float(2 ** 100)
    EPS = 1e-5

    NQ = 4
    QW = M // NQ
    QP = QW + 8
    S = NQ * 8
    SS = S + 1
    C = 5
    E = C * P
    NONE = 8192
    assert N == M and KD == 2

    x_v = x.rearrange("(g p r) d -> g p r d", p=P, r=R)
    n_v = neigh.rearrange("(g p r) d -> g p r d", p=P, r=R)
    adj_v = adj.rearrange("(g p r) m -> g p r m", p=P, r=R)
    adj_q = adj.rearrange("(g p r) (q w) -> g p r q w", p=P, r=R, q=NQ)
    out_v = out.rearrange("(g p r) d -> g p r d", p=P, r=R)

    ctx = ExitStack()
    with ctx:
        def sb(name, shape, dt=f32):
            return ctx.enter_context(nc.sbuf_tensor(name, shape, dt))

        def sem(name):
            return ctx.enter_context(nc.semaphore(name))

        table = nc.dram_tensor("table", (M + 1, TW), f32).ap()
        tab_w = table[0:M].rearrange("(g p r) d -> g p r d", p=P, r=R)
        tab_r = table[0:M].rearrange("(c p) d -> p c d", p=P)

        ident = sb("ident", [P, P])
        identb = sb("identb", [P, P], bf16)
        before = sb("before", [P, P], bf16)
        upto = sb("upto", [P, P], bf16)
        nextdiff = sb("nextdiff", [P, P], bf16)
        maskdiff = sb("maskdiff", [P, P], bf16)
        maskrow = sb("maskrow", [P, P], bf16)
        firstrow = sb("firstrow", [P, P], bf16)
        onesb = sb("onesb", [P, 512], bf16)
        onesf = sb("onesf", [P, P])
        meanw = sb("meanw", [P, 1])
        colno = sb("colno", [P, E], f16)
        colid = sb("colid", [P, C])
        quarter = sb("quarter", [P, 2 * SS], f16)
        ones_i = sb("ones_i", [P, 8], i32)
        restart = sb("restart", [P, R, SS])
        halfneg = sb("halfneg", [P, R])
        w1 = {s: sb(f"w1{s}", [P, KD, H]) for s in "nx"}
        w2 = {s: sb(f"w2{s}", [H, H]) for s in "nx"}
        ww = {s: sb(f"ww{s}", [P, KD, DO]) for s in "nx"}
        b1 = {s: sb(f"b1{s}", [H, 1]) for s in "nx"}
        b2x = sb("b2x", [H, 1])
        b2n = sb("b2n", [P, H])
        bvb = sb("bvb", [P, DO])
        bfb = sb("bfb", [P, DO])

        rows = [sb(f"rows{b}", [P, R, D]) for b in range(2)]
        hgrp = sb("hgrp", [P, R, D])
        rowsT = [sb(f"rowsT{b}", [P, KD, GW]) for b in range(2)]
        tanhT = sb("tanhT", [H, GW])
        tab = [sb(f"tab{b}", [P, R, TW]) for b in range(2)]
        vsum = sb("vsum", [P, R, DO])
        vmean = sb("vmean", [1, TW])
        left = [sb(f"left{b}", [P, R, DO]) for b in range(2)]
        xbias = [sb(f"xbias{b}", [P, R, DO]) for b in range(2)]
        stats = sb("stats", [P, R, 6])
        meanvar = sb("meanvar", [P, R, 2])
        vareps = sb("vareps", [P, R])
        rstd = sb("rstd", [P, R])
        shift = sb("shift", [P, R])
        xaT = sb("xaT", [H, N])
        xright = sb("xright", [P, NT, DO])

        adjt = [sb(f"adjt{r}", [P, NQ, QP], i32) for r in range(R)]
        found = sb("found", [P, R, S], u32)
        valid = sb("valid", [P, NT, SS])
        places = sb("places", [P, NT, 2 * SS], f16)
        adjsum = sb("adjsum", [P, NT, 2])
        sink = sb("sink", [P, 2, QW], bf16)
        cum = sb("cum", [P, R, SS])
        total = sb("total", [P, R], bf16)
        end = sb("end", [P, NT])
        passed = [sb(f"passed{r}", [P, E], bf16) for r in range(R)]
        diffs = sb("diffs", [P, NT, 2 * SS], f16)
        hit = sb("hit", [P, C, SS])
        entries = sb("entries", [P, C, SS])
        hitsum = sb("hitsum", [P, C])
        index = [sb(f"index{r}", [P, C], u32) for r in range(R)]

        shared = sb("shared", [P, M])
        cols = [shared[:, r * C * TW:(r + 1) * C * TW].rearrange("p (c w) -> p c w", c=C) for r in range(R)]
        xat = [sb(f"xat{r}", [H, P]) for r in range(R)]
        colsT = sb("colsT", [H, E])
        neg = shared[:, R * C * TW:R * C * TW + E]
        prob = [sb(f"prob{b}", [P, E]) for b in range(2)]
        probT = sb("probT", [P, E])
        smax = [sb(f"smax{b}", [P, 1]) for b in range(2)]
        snmax = [sb(f"snmax{b}", [P, 1]) for b in range(2)]
        ssum = [sb(f"ssum{b}", [P, 1]) for b in range(2)]
        sinv = [sb(f"sinv{i}", [P, 1]) for i in range(2)]

        counts = sb("counts", [P, NT])
        sums = sb("sums", [P, NT])
        slots = sb("slots", [P, NT])
        bad = sb("bad", [P, 2, NT])
        badsum = sb("badsum", [P, 1])
        flag = sb("flag", [1, 1], i32)

        d_adjt = [adjt[b][:].rearrange("p q w -> p (q w)")[:, 0:M] for b in range(2)]
        L = adjt[2][:].rearrange("p q w -> p (q w)")[:, 0:M].bitcast(f32)
        masked = adjt[3][:].rearrange("p q w -> p (q w)")[:, 0:M // 2].bitcast(bf16)
        naT = shared[0:H, :]
        V = xright
        na = hgrp[:].rearrange("p r d -> p (r d)").rearrange("p (c h) -> p c h", h=H)
        xag = tanhT
        negpart = [rowsT[0][:, k, :] for k in range(2)]
        PT = [rowsT[1][:, k, :] for k in range(2)]
        cmax = sb("cmax", [P, Q])
        rmax = sb("rmax", [P, 1])
        nmax = sb("nmax", [P, 1])
        rsum = sb("rsum", [P, 1])
        rinv = sb("rinv", [P, 1])
        xres = left[0]
        right = left[1]

        bankA = ctx.enter_context(nc.psum_tensor("bankA", [P, 1024], f32))
        bankB = ctx.enter_context(nc.psum_tensor("bankB", [P, 1024], f32))
        bankC = ctx.enter_context(nc.psum_tensor("bankC", [P, 1024], f32))
        bankD = ctx.enter_context(nc.psum_tensor("bankD", [P, 512], f32))
        bankF = ctx.enter_context(nc.psum_tensor("bankF", [P, 512], f32))
        psT = [bankA[:, 0:512], bankA[:, 512:1024]]
        psH = bankF[:]
        psW = [bankB[:, 0:512], bankB[:, 512:1024]]
        psS = [bankC[:, 0:512], bankC[:, 512:1024]]
        psStart, psEnd = bankD[:, 336:336 + R], bankD[:, 340:340 + R]
        psDiff = bankD[:, 344:344 + R // 2 * 2 * SS]
        psPick = bankD[:, 0:C * 2 * SS].rearrange("p (c s) -> p c s", c=C)
        psColsT = bankA[0:H, 0:E]
        psScore = bankB[:, 0:E]
        psProbT = bankC[:, 0:E]
        psOut = bankF[:, 0:DO]
        psCheck = bankD[:, 480:480 + NT]
        psMean = bankD[0:1, 384:384 + DO]
        dbank = [bankA[:, 0:512], bankA[:, 512:1024], bankB[:, 0:512], bankB[:, 512:1024], bankF[:]]

        weights_loaded = sem("weights_loaded")
        NVC = 8 + R
        NPC = 5 + R
        NWL = 12
        filled = sem("filled")
        consts_ready = sem("consts_ready")
        vec_consts = sem("vec_consts")

        class Side:

            def __init__(self, s):
                self.name = s
                self.rows_loaded = [sem(f"rows_loaded_{s}{b}") for b in range(2)]
                self.T0_copied = sem(f"T0_copied_{s}")
                self.T1_copied = sem(f"T1_copied_{s}")
                self.transposed = sem(f"transposed_{s}")
                self.hidden = sem(f"hidden_{s}")
                self.tanh_ready = sem(f"tanh_ready_{s}")
                self.wide = sem(f"wide_{s}")
                self.second = sem(f"second_{s}")
                self.wide_copied = sem(f"wide_copied_{s}")
                self.second_copied = sem(f"second_copied_{s}")
                self.stored = [sem(f"stored_{s}{b}") for b in range(2)]

        nb, xs = Side("n"), Side("x")
        vsum_added = sem("vsum_added")
        mean_ready = sem("mean_ready")
        vmean_copied = sem("vmean_copied")
        mean_stored = sem("mean_stored")
        stats_ready = sem("stats_ready")
        var_ready = sem("var_ready")
        vareps_ready = sem("vareps_ready")
        rstd_ready = sem("rstd_ready")
        shift_ready = sem("shift_ready")
        h_ready = sem("h_ready")
        xbias_ready = sem("xbias_ready")
        xright_loaded = sem("xright_loaded")
        xright_rest_loaded = sem("xright_rest_loaded")

        adj_loaded = [sem(f"adj_loaded{r}") for r in range(R)]
        quarter_found = sem("quarter_found")
        adj_summed = sem("adj_summed")
        valid_ready = sem("valid_ready")
        value_ready = sem("value_ready")
        scanned = sem("scanned")
        spare_valid = sem("spare_valid")
        spare_cum = sem("spare_cum")
        total_ready = sem("total_ready")
        ends_ready = sem("ends_ready")
        end_copied = sem("end_copied")
        columns_ready = sem("columns_ready")
        places_ready = sem("places_ready")
        diff_made = sem("diff_made")
        diffs_copied = sem("diffs_copied")
        passed_ready = sem("passed_ready")
        picked = sem("picked")
        entries_copied = sem("entries_copied")
        hits_summed = sem("hits_summed")
        index_ready = sem("index_ready")
        gathered = [sem(f"gathered{r}") for r in range(R)]
        xat_ready = [sem(f"xat_ready{r}") for r in range(R)]

        colsT_made = sem("colsT_made")
        colsT_copied = sem("colsT_copied")
        scored = sem("scored")
        neg_ready = sem("neg_ready")
        leaky_ready = sem("leaky_ready")
        nmax_ready = sem("nmax_ready")
        exp_ready = sem("exp_ready")
        probT_made = sem("probT_made")
        probT_copied = sem("probT_copied")
        summed_up = sem("summed_up")
        sinv_ready = sem("sinv_ready")
        result_ready = sem("result_ready")
        result_stored = sem("result_stored")

        check_step = sem("check_step")
        check_sum = sem("check_sum")
        flag_ready = sem("flag_ready")

        d_table = sem("d_table")
        d_naT = sem("d_naT")
        d_naT_copied = sem("d_naT_copied")
        d_adj = [sem(f"d_adj{b}") for b in range(2)]
        d_mask = sem("d_mask")
        d_xag = sem("d_xag")
        d_score = sem("d_score")
        d_neg = sem("d_neg")
        d_leaky = sem("d_leaky")
        d_rmax = sem("d_rmax")
        d_nmax = sem("d_nmax")
        d_exp = sem("d_exp")
        d_xpose = sem("d_xpose")
        d_pt = [sem(f"d_pt{k}") for k in range(2)]
        d_agg = sem("d_agg")
        d_rinv = sem("d_rinv")
        d_xres = sem("d_xres")
        d_right = sem("d_right")
        d_stored = sem("d_stored")

        pe_gate, dve_gate, pool_gate = sem("pe_gate"), sem("dve_gate"), sem("pool_gate")

        def ahead(g, r):
            return g + r // R, r % R

        def through(t):
            return t + 1 + R

        def group_through(g):
            return g + 2

        def halves_through(g, half):
            return 2 * g + half + 3

        def group_exists(g):
            return not isinstance(g, int) or 0 <= g < G

        EARLY = -6
        LISTS, DIFFS, ATTENTION, ALL = "l", "d", "a", "lda"

        def early(g, r):
            return isinstance(g, int) and R * g + r < R

        SEARCH = 3 * G
        PER_STEP = -(-2 * R * NQ // (SEARCH // 2 - 1))

        def quarters(k):
            return range(min(PER_STEP * k, 2 * R * NQ), min(PER_STEP * (k + 1), 2 * R * NQ))

        def group(g):
            return slice(R * g, R * (g + 1)) if isinstance(g, int) else bass.ds(R * g, R)

        def pair(g, half):
            t = R * g + R // 2 * half
            return slice(t, t + R // 2) if isinstance(g, int) else bass.ds(t, R // 2)

        def column(t):
            return slice(t, t + 1) if isinstance(t, int) else bass.ds(t, 1)

        def step_of(step, first, last):
            for t in range(first, last + 1):
                step(t // R, t % R)

        def exists(g, r):
            return not isinstance(g, int) or 0 <= R * g + r < NT

        block = ctx.enter_context(nc.Block())

        @block.sync
        def _(sp):
            def load(dst, src):
                sp.dma_start(dst, src).then_inc(weights_loaded, 16)

            for s, a, b_, c, d_ in (("n", Wn1, Wn2, Wv, bn1), ("x", Wx1, Wx2, Wfx, bx1)):
                load(w1[s][:], a.rearrange("(k p) h -> p k h", p=P))
                load(w2[s][:], b_)
                load(ww[s][:], c.rearrange("(k p) h -> p k h", p=P))
                load(b1[s][:], d_.rearrange("(h a) -> h a", a=1))
            load(b2x[:], bx2.rearrange("(h a) -> h a", a=1))
            load(b2n[:], bn2.partition_broadcast(P))
            load(bvb[:], bv.partition_broadcast(P))
            load(bfb[:], bfx.partition_broadcast(P))

            for r in range(R):
                if r >= 2:
                    sp.wait_ge(nb.hidden, r - 1)
                sp.dma_start(adjt[r][:, :, 0:QW], adj_q[0, :, r]).then_inc(adj_loaded[r], 16)

            def adj_loads(g):
                for r in range(R):
                    t = R * g + r
                    sp.wait_ge(quarter_found, NQ * (t + 1))
                    sp.wait_ge(adj_summed, 2 * (t + 1) + 1)
                    sp.dma_start(adjt[r][:, :, 0:QW], adj_q[g + 1, :, r]).then_inc(adj_loaded[r], 16)

            with sp.Fori(0, 2) as g:
                adj_loads(g)
            adj_loads(2)
            with sp.Fori(0, 2) as g:
                sp.dma_start(xright[:, bass.ds(R * g, R), :], x_v[g, :, :, DO:D]).then_inc(xright_loaded, 16)
            adj_loads(3)
            with sp.Fori(2, G) as g:
                sp.dma_start(xright[:, bass.ds(R * g, R), :], x_v[g, :, :, DO:D]).then_inc(xright_rest_loaded, 16)
            with sp.Fori(4, G - 1) as g:
                adj_loads(g)

            with sp.Fori(0, G) as g:
                sp.wait_ge(result_ready, through(R * g + R - 1))
                sp.dma_start(out_v[g, :, :, DO:D], xright[:, bass.ds(R * g, R), :]).then_inc(result_stored, 16)
            sp.wait_ge(result_stored, 16 * G)

            sp.wait_ge(flag_ready, 1)
            incomplete = sp.value_load(flag[0:1, 0:1], min_val=0, max_val=1)
            with sp.If(incomplete != 0):
                for b in range(2):
                    sp.wait_ge(xs.stored[b], 16 * (G // 2 + 1))
                sp.dma_start(V[:], tab_r[:, :, 0:DO]).then_inc(d_table, 16)
                sp.dma_start(na, tab_r[:, :, DO:TW]).then_inc(d_table, 16)
                for r in range(2):
                    sp.dma_start(d_adjt[r], adj_v[0, :, r, :]).then_inc(d_adj[r], 16)

                def dense_loads(g, last):
                    sp.wait_ge(d_right, R * g + 1)
                    sp.dma_start(xres[:], x_v[g, :, :, DO:D]).then_inc(d_xres, 16)
                    for r in range(2, R):
                        sp.wait_ge(d_mask, R * g + r - 1)
                        sp.dma_start(d_adjt[r % 2], adj_v[g, :, r, :]).then_inc(d_adj[r % 2], 16)
                    for r in range(0 if last else 2):
                        sp.wait_ge(d_mask, R * g + r + 3)
                        sp.dma_start(d_adjt[r], adj_v[g + 1, :, r, :]).then_inc(d_adj[r], 16)

                with sp.Fori(0, G - 1) as g:
                    dense_loads(g, False)
                dense_loads(G - 1, True)

        @block.gpsimd
        def _(pool):
            for b in range(2):
                pool.dma_start(rows[b][:], n_v[b]).then_inc(nb.rows_loaded[b], 16)

            def fill(t, v):
                nc.gpsimd.memset(t, v).then_inc(filled, 1)
                nfilled[0] += 1

            nfilled = [0]

            def select(m, op, fill_, base, mult=1, step=-1, n=P):
                pool.wait_ge(filled, nfilled[0])
                nc.gpsimd.affine_select(out=m, in_=m, compare_op=op, fill=fill_, base=base,
                                        pattern=[[step, n]], channel_multiplier=mult).then_inc(filled, 1)
                nfilled[0] += 1

            fill(ident[:], 0.0)
            select(ident[:], ALU.not_equal, 1.0, 0)
            fill(vsum[:], 0.0)

            def masks():
                for m in (identb, nextdiff, maskdiff, maskrow, firstrow, quarter):
                    fill(m[:], 0.0)
                fill(before[:], 1.0)
                fill(upto[:], 1.0)
                select(identb[:], ALU.not_equal, 1.0, 0)
                select(before[:], ALU.is_ge, 0.0, -1, -1, 1)
                select(upto[:], ALU.is_ge, 0.0, 0, -1, 1)
                select(nextdiff[:], ALU.not_equal, -1.0, 0)
                select(nextdiff[:], ALU.not_equal, 1.0, -1)
                select(maskdiff[:], ALU.not_equal, -BIG, 0)
                select(maskdiff[:], ALU.not_equal, BIG, 1)
                select(maskrow[:], ALU.not_equal, -BIG, 0, 1, 0)
                select(firstrow[:], ALU.not_equal, 1.0, 0, 1, 0)
                for q in range(NQ):
                    select(quarter[:, SS + 8 * q:SS + 8 * q + 8], ALU.not_equal, float(NONE - QW * q), 0, 1, 0, 8)
                select(quarter[:, SS + S:2 * SS], ALU.not_equal, float(NONE - M), 0, 1, 0, 1)

            def numbers():
                pool.wait_ge(filled, nfilled[0])
                nc.gpsimd.memset(maskrow[:, 0:1], 0.0).then_inc(consts_ready, 1)
                nc.gpsimd.iota(colno[:], pattern=[[1, E]], base=0, channel_multiplier=0,
                               allow_small_or_imprecise_dtypes=True).then_inc(consts_ready, 1)
                nc.gpsimd.iota(colid[:], pattern=[[P, C]], base=1, channel_multiplier=1,
                               allow_small_or_imprecise_dtypes=True).then_inc(consts_ready, 1)
                nc.gpsimd.memset(halfneg[:], -0.5).then_inc(consts_ready, 1)
                nc.gpsimd.memset(vmean[:], 0.0).then_inc(consts_ready, 1)
                for r in range(R):
                    nc.gpsimd.memset(cols[r], 0.0).then_inc(consts_ready, 1)

            def reload(j, b, src):
                pool.wait_ge(nb.transposed, 2 * (j + 1))
                pool.dma_start(rows[b][:], src).then_inc(nb.rows_loaded[b], 16)

            def add_values(j, b):
                pool.wait_ge(nb.wide_copied, j + 2)
                pool.wait_ge(vsum_added, j + 2)
                nc.gpsimd.tensor_tensor(vsum[:], vsum[:], tab[b][:, :, 0:DO], ALU.add).then_inc(vsum_added, 1)

            def rstds(j):
                pool.wait_ge(var_ready, R * (j + 1))
                pool.wait_ge(shift_ready, j + 1)
                pool.sem_inc(pool_gate, 1)
                nc.gpsimd.tensor_scalar(vareps[:], meanvar[:, :, 1], EPS, None, ALU.add).then_inc(vareps_ready, 1)
                pool.wait_ge(vareps_ready, j + 1)
                pool.wait_ge(h_ready, R * j + 1)
                nc.gpsimd.tensor_tensor(rstd[:], vareps[:], halfneg[:], ALU.pow).then_inc(rstd_ready, 1)

            def biases(j, b, it):
                pool.wait_ge(xs.rows_loaded[b], 16 * (it + 1))
                if j >= 2:
                    pool.wait_ge(xs.wide_copied, j)
                nc.gpsimd.tensor_tensor(xbias[b][:], rows[b][:, :, 0:DO],
                                        bfb[:].unsqueeze(1).to_broadcast([P, R, DO]),
                                        ALU.add).then_inc(xbias_ready, 1)

            def gather(g, r):
                t = R * g + r
                pool.wait_ge(index_ready, through(t))
                pool.wait_ge(summed_up, through(t - R))
                pool.sem_inc(pool_gate, 1)
                for c in range(C):
                    nc.gpsimd.indirect_dma_start(cols[r][:, c, :], None, table[:, :],
                                                 bass.IndirectOffsetOnAxis(ap=index[r][:, c:c + 1], axis=0),
                                                 bounds_check=M, oob_is_err=False).then_inc(gathered[r], 16)

            reload(0, 0, n_v[2])
            masks()
            pool.wait_ge(filled, nfilled[0])
            reload(1, 1, n_v[3])
            add_values(0, 0)
            numbers()
            add_values(1, 1)
            with pool.Fori(1, G // 2 - 1) as it:
                for b in range(2):
                    reload(2 * it + b, b, n_v[2 * it + 2 + b])
                    add_values(2 * it + b, b)
            add_values(G - 2, 0)
            pool.wait_ge(consts_ready, NPC)
            rstds(0)
            pool.wait_ge(weights_loaded, 16 * NWL)
            biases(0, 0, 0)
            add_values(G - 1, 1)
            rstds(1)
            biases(1, 1, 0)

            for j in range(G):
                b = j % 2
                if j + 2 < G:
                    rstds(j + 2)
                    biases(j + 2, b, j // 2 + 1)
                if j == G - R:
                    for k in range(2):
                        pool.wait_ge(nb.stored[k], 16 * (G // 2 + 1))
                    pool.wait_ge(mean_stored, 16)
                if j > G - R:
                    gather(0, j - (G - R) - 1)
            gather(0, R - 1)
            with pool.Fori(1, G) as g:
                for r in range(R):
                    gather(g, r)

        @block.tensor
        def _(pe):
            def transposes(sd, j, src):
                for k, copied in enumerate((sd.T0_copied, sd.T1_copied)):
                    pe.wait_ge(copied, j + 1)
                    for r in range(R):
                        last = nc.tensor.transpose(psT[k][:, r * P:(r + 1) * P], src[:, r, k * P:(k + 1) * P], ident[:])
                    last.then_inc(sd.transposed, 1)

            def hidden(sd, j, b):
                pe.wait_ge(sd.T0_copied, j + 2)
                pe.wait_ge(sd.T1_copied, j + 2)
                pe.wait_ge(sd.tanh_ready, j + 1)
                for k in range(KD):
                    last = nc.tensor.matmul(psH[0:H, :], w1[sd.name][:, k, :], rowsT[b][:, k, :],
                                            start=k == 0, stop=k == KD - 1)
                last.then_inc(sd.hidden, 1)

            def wide(sd, j, b):
                pe.wait_ge(sd.wide_copied, j + 1)
                for r in range(R):
                    for k in range(KD):
                        last = nc.tensor.matmul(psW[b][:, r * DO:(r + 1) * DO], rowsT[b][:, k, r * P:(r + 1) * P],
                                                ww[sd.name][:, k, :], start=k == 0, stop=k == KD - 1)
                last.then_inc(sd.wide, 1)

            def second_n(j, b):
                pe.wait_ge(nb.tanh_ready, j + 2)
                pe.wait_ge(nb.second_copied, j + 1)
                pe.sem_inc(pe_gate, 1)
                for r in range(R):
                    last = nc.tensor.matmul(psS[b][:, r * H:(r + 1) * H], tanhT[:, r * P:(r + 1) * P], w2["n"][:],
                                            start=True, stop=True)
                last.then_inc(nb.second, 1)

            def second_x(j, b):
                pe.wait_ge(xs.tanh_ready, j + 2)
                pe.wait_ge(xs.second_copied, j + 1)
                pe.sem_inc(pe_gate, 1)
                nc.tensor.matmul(psS[b][0:H, :], w2["x"][:], tanhT[:], start=True, stop=True).then_inc(xs.second, 1)

            for s in (picked, colsT_made, scored, probT_made, summed_up):
                pe.sem_inc(s, R)
            pe.sem_inc(ends_ready, 1)
            pe.sem_inc(diff_made, 2)
            pe.wait_ge(filled, 2)
            pe.wait_ge(nb.rows_loaded[0], 16)
            transposes(nb, 0, rows[0])
            pe.wait_ge(weights_loaded, 16 * NWL)

            def neigh_group(j, b, nxt, last):
                hidden(nb, j, b)
                if not last:
                    pe.wait_ge(nb.rows_loaded[1 - b], nxt)
                    transposes(nb, j + 1, rows[1 - b])
                wide(nb, j, b)
                second_n(j, b)

            with pe.Fori(0, G // 2 - 1) as it:
                for b in range(2):
                    neigh_group(2 * it + b, b, 16 * (it + 1 + b), False)
            for b in range(2):
                neigh_group(G - 2 + b, b, 16 * (G // 2), b == 1)

            pe.wait_ge(h_ready, R + 1)
            transposes(xs, 0, hgrp)

            pe.wait_ge(vsum_added, G + 2)
            pe.wait_ge(vec_consts, NVC)
            for r in range(R):
                last = nc.tensor.matmul(psMean, meanw[:], vsum[:, r, :], start=r == 0, stop=r == R - 1)
            last.then_inc(mean_ready, 1)
            pe.wait_ge(nb.wide_copied, G + 1)
            pe.wait_ge(nb.second_copied, G + 1)

            def x_group(j, b, last):
                hidden(xs, j, b)
                if not last:
                    pe.wait_ge(h_ready, R * (j + 2) + 1)
                    transposes(xs, j + 1, hgrp)
                if j >= G + EARLY:
                    step(*ahead(0, j - G), DIFFS)
                wide(xs, j, b)
                second_x(j, b)

            def ends(g):
                pe.wait_ge(total_ready, group_through(g))
                pe.wait_ge(hits_summed, C * through(R * g - 1))
                pe.sem_inc(pe_gate, 1)
                nc.tensor.matmul(psStart, before[:], total[:], start=True, stop=True)
                nc.tensor.matmul(psEnd, upto[:], total[:], start=True, stop=True).then_inc(ends_ready, 1)

            def diff(g, half):
                pe.wait_ge(places_ready, group_through(g))
                pe.wait_ge(end_copied, group_through(g))
                pe.wait_ge(hits_summed, C * through(R * (g - 1) + 2 * half + 3))
                pe.sem_inc(pe_gate, 1)
                nc.tensor.matmul(psDiff, nextdiff[:], places[:, pair(g, half), :], start=True, stop=True).then_inc(diff_made, 1)

            def pick(g, r):
                t = R * g + r
                pe.wait_ge(passed_ready, through(t))
                pe.wait_ge(diffs_copied, halves_through(g, r // 2))
                pe.wait_ge(hits_summed, C * through(t - 1))
                for c in range(C):
                    nc.tensor.matmul(psPick[:, c, :], passed[r][:, c * P:(c + 1) * P], diffs[:, t, :], start=True, stop=False)
                    nc.tensor.matmul(psPick[:, c, :], firstrow[:], places[:, t, :], start=False, stop=False)
                    last = nc.tensor.matmul(psPick[:, c, :], firstrow[:], quarter[:], start=False, stop=True)
                last.then_inc(picked, 1)

            def turn_cols(g, r):
                t = R * g + r
                pe.wait_ge(gathered[r], 16 * C * (g + 1))
                pe.wait_ge(colsT_copied, through(t - 1))
                for c in range(C):
                    last = nc.tensor.transpose(bankA[0:H, c * P:(c + 1) * P], cols[r][:, c, DO:TW], ident[:])
                last.then_inc(colsT_made, 1)

            def scores(g, r):
                t = R * g + r
                pe.wait_ge(colsT_copied, through(t))
                pe.wait_ge(xat_ready[r], 16 * (g + 1))
                pe.wait_ge(leaky_ready, through(t - 1))
                for a, b in ((0, 512), (512, E)):
                    nc.tensor.matmul(psScore[:, a:b], maskrow[:], onesb[:, 0:b - a], start=True, stop=False)
                    nc.tensor.matmul(psScore[:, a:b], maskdiff[:], passed[r][:, a:b], start=False, stop=False)
                    last = nc.tensor.matmul(psScore[:, a:b], xat[r][:], colsT[:, a:b], start=False, stop=True)
                last.then_inc(scored, 1)

            def turn_probs(g, r):
                t = R * g + r
                pe.wait_ge(exp_ready, through(t))
                pe.wait_ge(probT_copied, through(t - 1))
                for c in range(C):
                    last = nc.tensor.transpose(psProbT[:, c * P:(c + 1) * P], prob[r % 2][:, c * P:(c + 1) * P], ident[:])
                last.then_inc(probT_made, 1)

            def mix(g, r):
                t = R * g + r
                pe.wait_ge(probT_copied, through(t))
                pe.wait_ge(result_ready, through(t - 1))
                for c in range(C):
                    last = nc.tensor.matmul(psOut, probT[:, c * P:(c + 1) * P], cols[r][:, c, 0:DO],
                                            start=c == 0, stop=c == C - 1)
                last.then_inc(summed_up, 1)

            def step(g, r, parts=ALL):
                t1, t2, t4 = ahead(g, r + 1), ahead(g, r + 2), ahead(g, r + 4)
                if DIFFS in parts and r % 2 == 0 and group_exists(g + 1):
                    diff(g + 1, r // 2)
                if ATTENTION in parts and exists(*t1):
                    scores(*t1)
                if LISTS in parts and exists(*t4):
                    pick(*t4)
                if ATTENTION in parts and exists(g, r):
                    turn_probs(g, r)
                if ATTENTION in parts and exists(*t2):
                    turn_cols(*t2)
                if LISTS in parts and r == R - 1 and group_exists(g + 2):
                    ends(g + 2)
                if ATTENTION in parts and exists(g, r):
                    mix(g, r)

            for j in range(G + EARLY):
                x_group(j, j % 2, False)
            pe.wait_ge(vmean_copied, 1)
            pe.wait_ge(consts_ready, NPC)
            for j in range(G + EARLY, G):
                x_group(j, j % 2, j == G - 1)
                step(*ahead(0, j - G), LISTS)
            pe.wait_ge(xs.wide_copied, G + 1)
            pe.wait_ge(xs.second_copied, G + 1)
            for t in (-2, -1):
                step(*ahead(0, t), ATTENTION)

            with pe.Fori(0, 2) as it:
                for k in range(SEARCH // 2):
                    step(*ahead(SEARCH // 2 // R * it, k))
            step_of(step, SEARCH, NT - 4)
            pe.wait_ge(hits_summed, C * through(NT - 1))
            pe.wait_ge(check_step, 3)
            nc.tensor.matmul(psCheck, onesf[:], slots[:], start=True, stop=True).then_inc(check_sum, 1)
            step_of(step, NT - 3, NT - 3)
            pe.wait_ge(check_step, 6)
            nc.tensor.matmul(psCheck[:, 0:1], onesf[:], badsum[:], start=True, stop=True).then_inc(check_sum, 1)
            step_of(step, NT - 2, NT - 1)

            pe.wait_ge(flag_ready, 1)
            incomplete = pe.value_load(flag[0:1, 0:1], min_val=0, max_val=1)
            with pe.If(incomplete != 0):
                pe.wait_ge(result_ready, through(NT - 1))
                pe.wait_ge(d_table, 32)
                for q in range(Q):
                    if q >= 2:
                        pe.wait_ge(d_naT_copied, q - 1)
                    for c in range(4):
                        last = nc.tensor.transpose(dbank[q % 2][0:H, c * P:(c + 1) * P], na[:, 4 * q + c, :], ident[:])
                    last.then_inc(d_naT, 1)
                pe.wait_ge(d_naT_copied, Q)
                with pe.Fori(0, G) as g:
                    pe.wait_ge(d_xag, g + 1)
                    for r in range(R):
                        t = R * g + r
                        pe.wait_ge(d_mask, t + 1)
                        for q in range(Q):
                            pe.wait_ge(d_leaky, Q * t + q + 1)
                            nc.tensor.matmul(dbank[q % 2], identb[:], masked[:, q * 512:(q + 1) * 512], start=True, stop=False)
                            nc.tensor.matmul(dbank[q % 2], xag[:, r * P:(r + 1) * P], naT[:, q * 512:(q + 1) * 512],
                                             start=False, stop=True).then_inc(d_score, 1)

                        def weights_T(u):
                            pe.wait_ge(d_pt[u % 2], (Q // 2) * t + u // 2 + 1)
                            for c in range(4):
                                last = nc.tensor.transpose(dbank[2 + u % 2][:, c * P:(c + 1) * P],
                                                           L[:, (4 * u + c) * P:(4 * u + c + 1) * P], ident[:])
                            last.then_inc(d_xpose, 1)

                        pe.wait_ge(d_exp, t + 1)
                        pe.wait_ge(d_right, t + 1)
                        weights_T(0)
                        for u in range(Q):
                            if u + 1 < Q:
                                weights_T(u + 1)
                            pe.wait_ge(d_pt[u % 2], (Q // 2) * t + u // 2 + 2)
                            for c in range(4):
                                last = nc.tensor.matmul(dbank[4][:, 0:DO], PT[u % 2][:, c * P:(c + 1) * P], V[:, 4 * u + c, :],
                                                        start=(u == 0 and c == 0), stop=(u == Q - 1 and c == 3))
                        last.then_inc(d_agg, 1)

        @block.scalar
        def _(act):
            for s in (nb.T0_copied, nb.tanh_ready, xs.T0_copied, xs.tanh_ready, xs.second_copied, h_ready):
                act.sem_inc(s, 1)
            for s in (entries_copied, colsT_copied, neg_ready, exp_ready, probT_copied):
                act.sem_inc(s, R)
            for b in range(2):
                act.sem_inc(nb.stored[b], 16)
                act.sem_inc(xs.stored[b], 16)

            def add_up(g, r, half):
                if half == 0:
                    act.wait_ge(adj_loaded[r], 16 * (g + 1))
                act.wait_ge(adj_summed, 2 * (R * g + r) + half + 1)
                nc.scalar.activation(sink[:], adjt[r][:, 2 * half:2 * half + 2, 0:QW], ACT.Relu,
                                     accum_out=adjsum[:, R * g + r, half:half + 1]).then_inc(adj_summed, 1)

            def copy_T0(sd, j):
                act.wait_ge(sd.transposed, 2 * j + 1)
                nc.scalar.activation(rowsT[j % 2][:, 0, :], psT[0], ACT.Copy).then_inc(sd.T0_copied, 1)

            def tanh(sd, j):
                act.wait_ge(sd.hidden, j + 1)
                nc.scalar.activation(tanhT[:], psH[0:H, :], ACT.Tanh, bias=b1[sd.name][:]).then_inc(sd.tanh_ready, 1)

            def normalise(j):
                act.wait_ge(shift_ready, j + 2)
                if j > 0:
                    act.wait_ge(xs.transposed, 2 * j)
                for i in range(R):
                    nc.scalar.activation(hgrp[:, i, :], rows[j % 2][:, i, :], ACT.Relu, scale=rstd[:, i:i + 1],
                                         bias=shift[:, i:i + 1]).then_inc(h_ready, 1)

            copy_T0(nb, 0)
            act.wait_ge(weights_loaded, 16 * NWL)
            for j in range(G):
                g, r = j // R, j % R
                if j >= G - 2:
                    act.wait_ge(nb.transposed, 2 * (j + 1))
                    act.dma_start(rows[j % 2][:], x_v[j % 2]).then_inc(xs.rows_loaded[j % 2], 16)
                tanh(nb, j)
                if j + 1 < G:
                    copy_T0(nb, j + 1)
                else:
                    normalise(0)
                    copy_T0(xs, 0)
                    normalise(1)
                add_up(g, r, 0)
                add_up(g, r, 1)
                act.wait_ge(nb.second_copied, j + 2)
                act.wait_ge(nb.wide_copied, j + 2)
                act.dma_start(tab_w[j], tab[j % 2][:]).then_inc(nb.stored[j % 2], 16)

            def copy_colsT(g, r):
                t = R * g + r
                act.wait_ge(colsT_made, through(t))
                act.wait_ge(scored, through(t - 1))
                nc.scalar.activation(colsT[:], psColsT, ACT.Copy).then_inc(colsT_copied, 1)

            def negative_part(g, r):
                t = R * g + r
                act.wait_ge(scored, through(t))
                act.wait_ge(leaky_ready, through(t - 1))
                nc.scalar.activation(neg, psScore, ACT.Relu, scale=-0.99).then_inc(neg_ready, 1)

            def exponentials(g, r):
                t = R * g + r
                act.wait_ge(nmax_ready, through(t))
                act.wait_ge(sinv_ready, through(t - 2))
                nc.scalar.activation(prob[r % 2][:], prob[r % 2][:], ACT.Exp, bias=snmax[r % 2][:],
                                     accum_out=ssum[r % 2][:]).then_inc(exp_ready, 1)

            def copy_probT(g, r):
                t = R * g + r
                act.wait_ge(probT_made, through(t))
                act.wait_ge(summed_up, through(t - 1))
                nc.scalar.activation(probT[:], psProbT, ACT.Copy).then_inc(probT_copied, 1)

            def copy_entries(g, r):
                t = R * g + r
                act.wait_ge(picked, through(t))
                act.wait_ge(hits_summed, C * through(t - 1))
                nc.scalar.activation(entries[:], psPick[:, :, SS:2 * SS], ACT.Copy).then_inc(entries_copied, 1)

            def load_xat(g, r):
                t = R * g + r
                act.wait_ge(scored, through(t - R))
                if isinstance(g, int) and g == 0:
                    act.wait_ge(xs.second_copied, 2)
                act.dma_start(xat[r][:], xaT[:, bass.ds(t * P, P)]).then_inc(xat_ready[r], 16)

            def step(g, r, sums=(), parts=ALL):
                t1, t2, t4, t5 = ahead(g, r + 1), ahead(g, r + 2), ahead(g, r + 4), ahead(g, r + 5)
                if ATTENTION in parts and exists(*t1):
                    negative_part(*t1)
                if LISTS in parts and exists(*t4):
                    copy_entries(*t4)
                if (LISTS if early(*t5) else ATTENTION) in parts and exists(*t5):
                    load_xat(*t5)
                if ATTENTION in parts and exists(g, r):
                    copy_probT(g, r)
                if ATTENTION in parts and exists(*t2):
                    copy_colsT(*t2)
                for half in sums[0:-1]:
                    add_up(*half)
                if ATTENTION in parts and exists(*t1):
                    exponentials(*t1)
                for half in sums[-1:]:
                    add_up(*half)

            def reload(j):
                act.wait_ge(xbias_ready, j + 1)
                act.wait_ge(h_ready, R * (j + 1) + 1)
                act.dma_start(rows[j % 2][:], x_v[j + 2]).then_inc(xs.rows_loaded[j % 2], 16)

            reload(0)
            for j in range(G):
                g, r = (G + j) // R, j % R
                tanh(xs, j)
                if j == 0:
                    act.wait_ge(mean_ready, 1)
                    act.wait_ge(consts_ready, NPC)
                    nc.scalar.activation(vmean[:, 0:DO], psMean, ACT.Copy).then_inc(vmean_copied, 1)
                    act.wait_ge(vmean_copied, 1)
                    act.dma_start(table[M:M + 1, :], vmean[:]).then_inc(mean_stored, 16)
                if j + 1 < G:
                    copy_T0(xs, j + 1)
                if j + 3 < G:
                    reload(j + 1)
                if j < G - 1:
                    add_up(g, r, 0)
                act.wait_ge(xs.second, j + 1)
                nc.scalar.activation(xaT[:, j * GW:(j + 1) * GW], psS[j % 2][0:H, :], ACT.Identity,
                                     bias=b2x[:]).then_inc(xs.second_copied, 1)
                if j + 2 < G:
                    normalise(j + 2)
                if j >= G + EARLY:
                    step(*ahead(0, j - G), parts=LISTS)
                if j < G - 1:
                    add_up(g, r, 1)
                act.wait_ge(xs.wide_copied, j + 2)
                act.dma_start(out_v[j, :, :, 0:DO], left[j % 2][:]).then_inc(xs.stored[j % 2], 16)
            act.wait_ge(xs.second_copied, G + 1)
            for t in (-2, -1):
                step(*ahead(0, t), [(G // 2 - 1, R - 1, t + 2)], ATTENTION)

            with act.Fori(0, 2) as it:
                for k in range(SEARCH // 2):
                    sums = [(*ahead(G // 2 + 2 * it, n // NQ), n % NQ // 2) for n in quarters(k) if n % 2]
                    step(*ahead(SEARCH // 2 // R * it, k), sums)
            step_of(step, SEARCH, NT - 1)

            for b in range(2):
                act.wait_ge(xs.stored[b], 16 * (G // 2 + 1))
            act.wait_ge(flag_ready, 1)
            incomplete = act.value_load(flag[0:1, 0:1], min_val=0, max_val=1)
            with act.If(incomplete != 0):
                act.sem_inc(d_pt[0], 1)
                act.sem_inc(d_stored, 16)
                with act.Fori(0, G) as g:
                    nc.scalar.activation(xag[:], xaT[:, bass.ds(g * GW, GW)], ACT.Copy).then_inc(d_xag, 1)
                    for r in range(R):
                        t = R * g + r
                        for q in range(Q):
                            act.wait_ge(d_score, Q * t + q + 1)
                            act.wait_ge(d_leaky, Q * t + q + 1)
                            nc.scalar.activation(negpart[q % 2], dbank[q % 2], ACT.Relu, scale=-0.99).then_inc(d_neg, 1)
                        act.wait_ge(d_nmax, t + 1)
                        act.wait_ge(d_rinv, t + 1)
                        nc.scalar.activation(L, L, ACT.Exp, bias=nmax[:], accum_out=rsum[:]).then_inc(d_exp, 1)
                        for u in range(0, Q, 2):
                            act.wait_ge(d_xpose, Q * t + u + 1)
                            nc.scalar.activation(PT[0], dbank[2], ACT.Copy).then_inc(d_pt[0], 1)
                    act.wait_ge(d_right, R * (g + 1) + 1)
                    act.wait_ge(result_stored, 16 * G)
                    act.dma_start(out_v[g, :, :, DO:D], right[:]).then_inc(d_stored, 16)
                act.wait_ge(d_stored, 16 * (G + 1))

        @block.vector
        def _(dve):
            for s in (nb.T1_copied, nb.wide_copied, nb.second_copied, xs.T1_copied, xs.wide_copied, shift_ready,
                      adj_summed):
                dve.sem_inc(s, 1)
            for s in (scanned, total_ready, spare_cum, spare_valid, end_copied, columns_ready, places_ready):
                dve.sem_inc(s, 1)
            dve.sem_inc(diffs_copied, 2)
            dve.sem_inc(hits_summed, R * C)
            for s in (passed_ready, index_ready, leaky_ready, nmax_ready, sinv_ready, result_ready):
                dve.sem_inc(s, R)
            dve.sem_inc(vsum_added, 2)
            for t, v in [(ones_i[:], 1), (restart[:, :, 0:1], 0.0), (restart[:, :, 1:SS], 1.0),
                         (valid[:, :, S:SS], 0.0), (onesb[:], 1.0), (onesf[:], 1.0), (meanw[:], 1.0 / M),
                         (places[:, :, SS + S:2 * SS], 0.0)] + [(adjt[r][:, :, QW:QP], 1) for r in range(R)]:
                nc.vector.memset(t, v).then_inc(vec_consts, 1)

            def find(g, r, q):
                if q == 0:
                    dve.wait_ge(adj_loaded[r], 16 * (g + 1))
                    if r == 0:
                        dve.wait_ge(valid_ready, g + 1)
                        dve.wait_ge(value_ready, g + 1)
                    dve.sem_inc(dve_gate, 1)
                nc.vector.max_index(found[:, r, 8 * q:8 * q + 8], ones_i[:], adjt[r][:, q, :]).then_inc(quarter_found, 1)

            def keep(g):
                dve.wait_ge(quarter_found, NQ * R * (g + 1))
                nc.vector.tensor_scalar(valid[:, group(g), 0:S], found[:], float(QW), None, ALU.is_lt).then_inc(valid_ready, 1)
                nc.vector.tensor_scalar(places[:, group(g), SS:SS + S], found[:], -1.0, None, ALU.mult).then_inc(value_ready, 1)

            def copy_T1(sd, j):
                dve.wait_ge(sd.transposed, 2 * j + 2)
                nc.vector.tensor_copy(rowsT[j % 2][:, 1, :], psT[1]).then_inc(sd.T1_copied, 1)

            def moments(j):
                dve.wait_ge(xs.rows_loaded[j % 2], 16 * (j // 2 + 1))
                for i in range(R):
                    nc.vector.bn_stats(stats[:, i, :], rows[j % 2][:, i, :]).then_inc(stats_ready, 1)
                dve.wait_ge(stats_ready, R * (j + 1))
                for i in range(R):
                    nc.vector.bn_aggr(meanvar[:, i, :], stats[:, i, :]).then_inc(var_ready, 1)

            def shifts(j):
                dve.wait_ge(rstd_ready, j + 1)
                dve.wait_ge(var_ready, R * (j + 1))
                if j > 0:
                    dve.wait_ge(h_ready, R * j + 1)
                nc.vector.scalar_tensor_tensor(shift[:], meanvar[:, :, 0], -1.0, rstd[:], ALU.mult,
                                               ALU.mult).then_inc(shift_ready, 1)

            dve.sem_inc(valid_ready, 1)
            dve.sem_inc(value_ready, 1)
            copy_T1(nb, 0)
            dve.wait_ge(vec_consts, NVC)
            dve.wait_ge(weights_loaded, 16 * NWL)
            for j in range(G):
                g, r, b = j // R, j % R, j % 2
                find(g, r, 0)
                if j + 1 < G:
                    copy_T1(nb, j + 1)
                else:
                    shifts(0)
                    moments(1)
                find(g, r, 1)
                dve.wait_ge(nb.wide, j + 1)
                dve.wait_ge(nb.stored[b], 16 * (j // 2 + 1))
                dve.wait_ge(vsum_added, j + 1)
                nc.vector.tensor_tensor(tab[b][:, :, 0:DO], psW[b].rearrange("p (r d) -> p r d", r=R),
                                        bvb[:].unsqueeze(1).to_broadcast([P, R, DO]), ALU.add).then_inc(nb.wide_copied, 1)
                dve.wait_ge(nb.second, j + 1)
                nc.vector.tensor_tensor(tab[b][:, :, DO:TW], psS[b][:, 0:R * H].rearrange("p (r d) -> p r d", r=R),
                                        b2n[:].unsqueeze(1).to_broadcast([P, R, H]), ALU.add).then_inc(nb.second_copied, 1)
                find(g, r, 2)
                if j == G - 2:
                    moments(0)
                if j == G - 1:
                    copy_T1(xs, 0)
                    shifts(1)
                find(g, r, 3)
                if r == R - 1:
                    keep(g)

            def count(g):
                dve.wait_ge(valid_ready, group_through(g))
                dve.wait_ge(end_copied, group_through(g - 1))
                dve.wait_ge(columns_ready, group_through(g - 1))
                flat = slice(R * SS * g, R * SS * (g + 1)) if isinstance(g, int) else bass.ds(R * SS * g, R * SS)
                nc.vector.tensor_tensor_scan(cum[:].rearrange("p r s -> p (r s)"), restart[:].rearrange("p r s -> p (r s)"),
                                             valid[:].rearrange("p t s -> p (t s)")[:, flat], 0.0, ALU.mult,
                                             ALU.add).then_inc(scanned, 1)
                dve.wait_ge(scanned, group_through(g))
                nc.vector.tensor_scalar(total[:], cum[:, :, S - 1], 1.0, None, ALU.max).then_inc(total_ready, 1)
                nc.vector.tensor_scalar(cum[:, :, S], cum[:, :, S - 1], 1.0, None, ALU.max).then_inc(spare_cum, 1)
                nc.vector.tensor_scalar(valid[:, group(g), S], cum[:, :, S - 1], 0.0, None, ALU.is_equal).then_inc(spare_valid, 1)

            def place(g):
                dve.wait_ge(ends_ready, group_through(g))
                dve.wait_ge(spare_cum, group_through(g))
                dve.wait_ge(spare_valid, group_through(g))
                nc.vector.tensor_tensor(cum[:], cum[:], psStart.unsqueeze(2).to_broadcast([P, R, SS]),
                                        ALU.add).then_inc(columns_ready, 1)
                nc.vector.tensor_copy(end[:, group(g)], psEnd).then_inc(end_copied, 1)
                dve.wait_ge(value_ready, group_through(g))
                dve.wait_ge(columns_ready, group_through(g))
                nc.vector.tensor_tensor(places[:, group(g), 0:SS], cum[:], valid[:, group(g), :], ALU.mult).then_inc(places_ready, 1)

            def copy_diffs(g, half):
                dve.wait_ge(diff_made, halves_through(g, half))
                nc.vector.tensor_copy(diffs[:, pair(g, half), :],
                                      psDiff.rearrange("p (r s) -> p r s", r=R // 2)).then_inc(diffs_copied, 1)

            def pass_by(g, r):
                t = R * g + r
                dve.wait_ge(end_copied, group_through(g))
                dve.wait_ge(scored, through(t - R))
                nc.vector.tensor_scalar(passed[r][:], colno[:], end[:, column(t)], None, ALU.is_ge).then_inc(passed_ready, 1)

            def list_up(g, r):
                t = R * g + r
                dve.wait_ge(entries_copied, through(t))
                for c in range(C):
                    nc.vector.scalar_tensor_tensor(hit[:, c, :], psPick[:, c, 0:SS], colid[:, c:c + 1], entries[:, c, :],
                                                   ALU.is_equal, ALU.mult,
                                                   accum_out=hitsum[:, c:c + 1]).then_inc(hits_summed, 1)

            def write_index(g, r):
                t = R * g + r
                dve.wait_ge(hits_summed, C * through(t))
                dve.wait_ge(colsT_made, through(t - R))
                nc.vector.tensor_scalar(index[r][:], hitsum[:], -1.0, float(NONE), ALU.mult, ALU.add).then_inc(index_ready, 1)

            def leaky(g, r):
                t = R * g + r
                b = r % 2
                dve.wait_ge(neg_ready, through(t))
                dve.wait_ge(probT_made, through(t - 2))
                dve.sem_inc(dve_gate, 1)
                nc.vector.tensor_tensor_reduce(out=prob[b][:], in0=psScore, in1=neg, scale=1.0, scalar=-3.0e38,
                                               op0=ALU.add, op1=ALU.max, accum_out=smax[b][:]).then_inc(leaky_ready, 1)

            def negate(g, r):
                t = R * g + r
                b = r % 2
                dve.wait_ge(leaky_ready, through(t))
                nc.vector.tensor_scalar(snmax[b][:], smax[b][:], -1.0, None, ALU.mult).then_inc(nmax_ready, 1)

            def invert(g, r):
                t = R * g + r
                dve.wait_ge(exp_ready, through(t))
                dve.wait_ge(result_ready, through(t - 2))
                nc.vector.reciprocal(sinv[r % 2][:], ssum[r % 2][:]).then_inc(sinv_ready, 1)

            def result(g, r):
                t = R * g + r
                dve.wait_ge(sinv_ready, through(t))
                dve.wait_ge(summed_up, through(t))
                nc.vector.scalar_tensor_tensor(xright[:, t, :], psOut, sinv[r % 2][:], xright[:, t, :], ALU.mult,
                                               ALU.add).then_inc(result_ready, 1)

            def step(g, r, finds=(), parts=ALL):
                t1, t4, t5 = ahead(g, r + 1), ahead(g, r + 4), ahead(g, r + 5)

                def search(part):
                    for z, place_, q in finds[part:part + 1]:
                        find(z, place_, q)
                        if place_ == R - 1 and q == NQ - 1:
                            keep(z)

                if DIFFS in parts and r % 2 == 0 and group_exists(g + 1):
                    copy_diffs(g + 1, r // 2)
                search(0)
                if ATTENTION in parts and exists(*t1):
                    leaky(*t1)
                if ATTENTION in parts and exists(g, r):
                    invert(g, r)
                if ATTENTION in parts and exists(*t1):
                    negate(*t1)
                if LISTS in parts and exists(*t4):
                    list_up(*t4)
                if not finds and LISTS in parts and exists(*t4):
                    write_index(*t4)
                search(1)
                if finds and LISTS in parts and exists(*t4):
                    write_index(*t4)
                if LISTS in parts and r == R - 1 and group_exists(g + 2):
                    place(g + 2)
                if (LISTS if early(*t5) else ATTENTION) in parts and exists(*t5):
                    pass_by(*t5)
                search(2)
                if ATTENTION in parts and exists(g, r):
                    result(g, r)
                if LISTS in parts and r == R - 2 and group_exists(g + 2):
                    count(g + 2)

            dve.wait_ge(consts_ready, NPC)
            for j in range(G):
                g, r, b = (G + j) // R, j % R, j % 2
                searched = () if j == G - 1 else range(NQ)
                for q in searched[0:1]:
                    find(g, r, q)
                if j + 1 < G:
                    copy_T1(xs, j + 1)
                if j + 2 < G:
                    moments(j + 2)
                for q in searched[1:2]:
                    find(g, r, q)
                dve.wait_ge(xs.wide, j + 1)
                dve.wait_ge(xbias_ready, j + 1)
                dve.wait_ge(xs.stored[b], 16 * (j // 2 + 1))
                nc.vector.tensor_tensor(left[b][:], psW[b].rearrange("p (r d) -> p r d", r=R), xbias[b][:],
                                        ALU.add).then_inc(xs.wide_copied, 1)
                if j + 2 < G:
                    shifts(j + 2)
                if j >= G + EARLY:
                    step(*ahead(0, j - G), parts=DIFFS)
                for q in searched[2:]:
                    find(g, r, q)
                if r == R - 1 and searched:
                    keep(g)
                if j >= G + EARLY:
                    step(*ahead(0, j - G), parts=LISTS)

            dve.wait_ge(xright_loaded, 16 * 2)
            for t in (-2, -1):
                step(*ahead(0, t), [(G // 2 - 1, R - 1, NQ // 2 * (t + 2) + q) for q in range(NQ // 2)], ATTENTION)
            with dve.Fori(0, 2) as it:
                for k in range(SEARCH // 2):
                    finds = [(*ahead(G // 2 + 2 * it, n // NQ), n % NQ) for n in quarters(k)]
                    if k == 2 * R:
                        dve.wait_ge(xright_rest_loaded, 16 * (G - 2))
                    step(*ahead(SEARCH // 2 // R * it, k), finds)

            step_of(step, SEARCH, SEARCH)
            dve.wait_ge(valid_ready, G + 1)
            nc.vector.tensor_reduce(counts[:], valid[:, :, 0:S], AX.X, ALU.add).then_inc(check_step, 1)
            dve.wait_ge(adj_summed, 2 * NT + 1)
            nc.vector.tensor_tensor(sums[:], adjsum[:, :, 0], adjsum[:, :, 1], ALU.add).then_inc(check_step, 1)
            dve.wait_ge(check_step, 2)
            nc.vector.tensor_scalar(slots[:], counts[:], 1.0, None, ALU.max).then_inc(check_step, 1)
            nc.vector.tensor_tensor(bad[:, 0, :], sums[:], counts[:], ALU.not_equal).then_inc(check_step, 1)
            step_of(step, SEARCH + 1, NT - 4)
            dve.wait_ge(check_sum, 1)
            nc.vector.tensor_scalar(bad[:, 1, :], psCheck, float(E), None, ALU.is_gt).then_inc(check_step, 1)
            dve.wait_ge(check_step, 5)
            nc.vector.tensor_reduce(badsum[:], bad[:], AX.XY, ALU.add).then_inc(check_step, 1)
            step_of(step, NT - 3, NT - 3)
            dve.wait_ge(check_sum, 2)
            nc.vector.tensor_scalar(flag[:], psCheck[0:1, 0:1], 0.0, None, ALU.is_gt).then_inc(flag_ready, 1)
            step_of(step, NT - 2, NT - 1)

            dve.wait_ge(flag_ready, 1)
            incomplete = dve.value_load(flag[0:1, 0:1], min_val=0, max_val=1)
            with dve.If(incomplete != 0):
                dve.sem_inc(d_leaky, 2)
                dve.sem_inc(d_pt[1], 1)
                dve.sem_inc(d_right, 1)
                dve.sem_inc(d_rinv, 1)
                for q in range(Q):
                    dve.wait_ge(d_naT, q + 1)
                    nc.vector.tensor_copy(naT[:, q * 512:(q + 1) * 512], dbank[q % 2][0:H, :]).then_inc(d_naT_copied, 1)
                with dve.Fori(0, G) as g:
                    for r in range(R):
                        t = R * g + r
                        dve.wait_ge(d_adj[r % 2], 32 * g + 16 * (r // 2) + 16)
                        nc.vector.tensor_scalar(masked, d_adjt[r % 2], 0.0, -BIG, ALU.is_le, ALU.mult).then_inc(d_mask, 1)
                        for q in range(Q):
                            dve.wait_ge(d_neg, Q * t + q + 1)
                            dve.sem_inc(dve_gate, 1)
                            nc.vector.tensor_tensor_reduce(out=L[:, q * 512:(q + 1) * 512], in0=dbank[q % 2],
                                                           in1=negpart[q % 2], scale=1.0, scalar=-3.0e38,
                                                           op0=ALU.add, op1=ALU.max,
                                                           accum_out=cmax[:, q:q + 1]).then_inc(d_leaky, 1)
                        dve.wait_ge(d_leaky, Q * (t + 1) + 2)
                        nc.vector.tensor_reduce(rmax[:], cmax[:], AX.X, ALU.max).then_inc(d_rmax, 1)
                        dve.wait_ge(d_rmax, t + 1)
                        nc.vector.tensor_scalar(nmax[:], rmax[:], -1.0, None, ALU.mult).then_inc(d_nmax, 1)
                        for u in range(1, Q, 2):
                            dve.wait_ge(d_xpose, Q * t + u + 1)
                            nc.vector.tensor_copy(PT[1], dbank[3]).then_inc(d_pt[1], 1)
                        dve.wait_ge(d_exp, t + 1)
                        nc.vector.reciprocal(rinv[:], rsum[:]).then_inc(d_rinv, 1)
                        dve.wait_ge(d_agg, t + 1)
                        dve.wait_ge(d_rinv, t + 2)
                        if r == 0:
                            dve.wait_ge(d_xres, 16 * (g + 1))
                            dve.wait_ge(d_stored, 16 * (g + 1))
                        nc.vector.scalar_tensor_tensor(right[:, r, :], dbank[4][:, 0:DO], rinv[:], xres[:, r, :],
                                                       ALU.mult, ALU.add).then_inc(d_right, 1)


_INS = ["x", "adj"] + ["L0_gnn_" + n for n in
        ("neigh", "Wx1", "bx1", "Wx2", "bx2", "Wn1", "bn1", "Wn2", "bn2", "Wv", "bv", "Wfx", "bfx")]


def kernel(**inputs):
    import numpy as np
    import concourse.bacc as bacc
    from concourse.bass_utils import run_bass_kernel_spmd

    nc = bacc.Bacc("TRN2", target_bir_lowering=False, num_devices=1)
    arrays, args = {}, []
    for name in _INS:
        a = np.ascontiguousarray(inputs[name])
        arrays[name] = a
        args.append(nc.dram_tensor(name, a.shape, mybir.dt.from_np(a.dtype), kind="ExternalInput").ap())
    args.append(nc.dram_tensor("out", arrays["x"].shape, mybir.dt.float32, kind="ExternalOutput").ap())
    preln_gnn(nc, *args)
    return run_bass_kernel_spmd(nc, [arrays], core_ids=[0]).results[0]["out"]
```
